# Optimizing a Trainium2 kernel written in Bass

```python
import numpy as np
import jax
import jax.numpy as jnp

def _softmax(x, axis=-1):
    return jax.nn.softmax(x, axis=axis)

def _gelu(x):
    return jax.nn.gelu(x, approximate=True)

def _silu(x):
    return jax.nn.silu(x)

def _sigmoid(x):
    return jax.nn.sigmoid(x)

def _layernorm(x, axis=-1, eps=1e-05):
    m = jnp.mean(x, axis=axis, keepdims=True)
    v = jnp.var(x, axis=axis, keepdims=True)
    return (x - m) / jnp.sqrt(v + eps)

def _scatter_add(tgt, idx, src, axis=0):
    return tgt.at[idx].add(src)

def _segment_sum(src, seg, n):
    return jax.ops.segment_sum(src, seg, n)
kernel_name = 'mk_xattn_ffn_d1_seqx_r4_dc8fda'

def setup_inputs(seed: int=0):
    np.random.seed(seed)
    _w = jnp.asarray

    def _rec_inputs():
        import jax
        import jax.numpy as jnp
        _rk = jax.random.key(seed)
        x = 7.22e-05 + 1 * jax.random.normal(jax.random.fold_in(_rk, 1), (16, 512, 256), jnp.float32)
        _lenS = 512 - jax.random.randint(jax.random.fold_in(_rk, 7), (16,), 0, max(1, 512 // 4) + 1, jnp.int32)
        _lenS2 = 64 - jax.random.randint(jax.random.fold_in(_rk, 8), (16,), 0, max(1, 64 // 4) + 1, jnp.int32)
        _ctx_1024P = jax.random.normal(jax.random.fold_in(_rk, 11), (16, 16, 256), jnp.float32)
        _ctx_1024c = jax.random.dirichlet(jax.random.fold_in(_rk, 511), 0.3 * jnp.ones((16,), jnp.float32), (16, 64))
        _ctx_1024t = jnp.einsum('bsk,bkd->bsd', _ctx_1024c, _ctx_1024P)
        _ctx_1024t = _ctx_1024t * jax.lax.rsqrt(jnp.mean(jnp.square(_ctx_1024t)) + 1e-12) * 0.953939
        ctx_1024 = 4.13588e-05 + 0.999923 * (_ctx_1024t + 0.3 * jax.random.normal(jax.random.fold_in(_rk, 611), (16, 64, 256), jnp.float32))
        _validS = jnp.arange(512)[None, :] < _lenS[:, None]
        _validS2 = jnp.arange(64)[None, :] < _lenS2[:, None]
        _causal = jnp.tril(jnp.ones((512, 512), dtype=bool))
        mask_SxS2_bk1 = jnp.broadcast_to(_validS2[0:1, :], (512, 64))
        return (x, ctx_1024, mask_SxS2_bk1)
    x, ctx_1024, mask_SxS2_bk1 = _rec_inputs()

    def _L0_xattn_setup():
        import jax, jax.numpy as jnp
        import numpy as np
        B, S, D, H = (4, 512, 256, 16)
        HD = D // H
        key = jax.random.key(seed)
        ks = jax.random.split(key, 16)
        inv = 1.0 / np.sqrt(D)
        inv_hd = 1.0 / np.sqrt(D)
        inp = {'query': jax.random.normal(ks[0], (B, S, D), jnp.float32), 'key': jax.random.normal(ks[1], (B, S, D), jnp.float32), 'value': jax.random.normal(ks[2], (B, S, D), jnp.float32), 'mask': jnp.triu(jnp.ones((S, S), jnp.bool_), k=1), 'Wq': jax.random.normal(ks[3], (D, D), jnp.float32) * inv, 'Wk': jax.random.normal(ks[4], (D, D), jnp.float32) * inv, 'Wv': jax.random.normal(ks[5], (D, D), jnp.float32) * inv, 'wq_h': jax.random.normal(ks[6], (D, HD), jnp.float32) * inv_hd, 'bq_h': jax.random.normal(ks[7], (HD,), jnp.float32) * inv_hd, 'wk_h': jax.random.normal(ks[8], (D, HD), jnp.float32) * inv_hd, 'bk_h': jax.random.normal(ks[9], (HD,), jnp.float32) * inv_hd, 'wv_h': jax.random.normal(ks[10], (D, HD), jnp.float32) * inv_hd, 'bv_h': jax.random.normal(ks[11], (HD,), jnp.float32) * inv_hd, 'Wo': jax.random.normal(ks[12], (D, D), jnp.float32) * inv}
        return inp
    _L0_xattn_all = _L0_xattn_setup()
    _L0_xattn_in = {k: v for k, v in _L0_xattn_all.items() if k in ('Wq', 'Wk', 'Wv', 'wq_h', 'bq_h', 'wk_h', 'bk_h', 'wv_h', 'bv_h', 'Wo')}
    del _L0_xattn_all

    def _L0_ffn_setup():
        import jax, jax.numpy as jnp
        import numpy as np

        def _binarize(w):
            alpha = jax.lax.stop_gradient(jnp.mean(jnp.abs(w), axis=1, keepdims=True))
            bw = alpha * jnp.sign(w)
            return w + jax.lax.stop_gradient(bw - w)
        key = jax.random.key(seed)
        k1, k2, k3, k4, k5 = jax.random.split(key, 5)
        D, H = (256, 1024)
        x = jax.random.normal(k1, (64, 196, D), dtype=jnp.float32)
        w1 = jax.random.normal(k2, (H, D), dtype=jnp.float32) * 0.02
        b1 = jax.random.normal(k3, (H,), dtype=jnp.float32) * 0.02
        w2 = jax.random.normal(k4, (D, H), dtype=jnp.float32) * 0.02
        b2 = jax.random.normal(k5, (D,), dtype=jnp.float32) * 0.02
        return {'x': x, 'w1': w1, 'b1': b1, 'w2': w2, 'b2': b2}
    _L0_ffn_all = _L0_ffn_setup()
    _L0_ffn_in = {k: v for k, v in _L0_ffn_all.items() if k in ('w1', 'b1', 'w2', 'b2')}
    del _L0_ffn_all
    return {'x': x, 'ctx_1024': ctx_1024, 'mask_SxS2_bk1': mask_SxS2_bk1, 'L0_xattn_Wq': _L0_xattn_in['Wq'], 'L0_xattn_Wk': _L0_xattn_in['Wk'], 'L0_xattn_Wv': _L0_xattn_in['Wv'], 'L0_xattn_wq_h': _L0_xattn_in['wq_h'], 'L0_xattn_bq_h': _L0_xattn_in['bq_h'], 'L0_xattn_wk_h': _L0_xattn_in['wk_h'], 'L0_xattn_bk_h': _L0_xattn_in['bk_h'], 'L0_xattn_wv_h': _L0_xattn_in['wv_h'], 'L0_xattn_bv_h': _L0_xattn_in['bv_h'], 'L0_xattn_Wo': _L0_xattn_in['Wo'], 'L0_ffn_w1': _L0_ffn_in['w1'], 'L0_ffn_b1': _L0_ffn_in['b1'], 'L0_ffn_w2': _L0_ffn_in['w2'], 'L0_ffn_b2': _L0_ffn_in['b2']}

def reference(x, ctx_1024, mask_SxS2_bk1, L0_xattn_Wq, L0_xattn_Wk, L0_xattn_Wv, L0_xattn_wq_h, L0_xattn_bq_h, L0_xattn_wk_h, L0_xattn_bk_h, L0_xattn_wv_h, L0_xattn_bv_h, L0_xattn_Wo, L0_ffn_w1, L0_ffn_b1, L0_ffn_w2, L0_ffn_b2):
    import jax
    import jax.numpy as jnp

    def _L0_xattn_ref(query, key, value, mask, Wq, Wk, Wv, wq_h, bq_h, wk_h, bk_h, wv_h, bv_h, Wo):
        import jax, jax.numpy as jnp
        import numpy as np
        B, S, D, H = (4, 512, 256, 16)
        HD = D // H
        q = jnp.einsum('bsd,de->bse', query, Wq)
        k = jnp.einsum('bsd,de->bse', key, Wk)
        v = jnp.einsum('bsd,de->bse', value, Wv)
        qh = jnp.einsum('bsd,dh->bsh', q, wq_h) + bq_h
        kh = jnp.einsum('bsd,dh->bsh', k, wk_h) + bk_h
        vh = jnp.einsum('bsd,dh->bsh', v, wv_h) + bv_h
        scores = jnp.einsum('bsh,bth->bst', qh, kh) / jnp.sqrt(jnp.float32(HD))
        scores = jnp.where(mask, jnp.float32(-1000000000.0), scores)
        attn = jax.nn.softmax(scores, axis=-1)
        out_h = jnp.einsum('bst,bth->bsh', attn, vh)
        out = jnp.tile(out_h, (1, 1, H))
        return jnp.einsum('bsd,de->bse', out, Wo)

    def _L0_ffn_ref(x, w1, b1, w2, b2):
        import jax, jax.numpy as jnp
        import numpy as np

        def _binarize(w):
            alpha = jax.lax.stop_gradient(jnp.mean(jnp.abs(w), axis=1, keepdims=True))
            bw = alpha * jnp.sign(w)
            return w + jax.lax.stop_gradient(bw - w)
        bw1 = _binarize(w1)
        h = jnp.einsum('bsd,hd->bsh', x, bw1) + b1
        h = jax.nn.gelu(h, approximate=False)
        bw2 = _binarize(w2)
        out = jnp.einsum('bsh,dh->bsd', h, bw2) + b2
        return out
    x = x + _L0_xattn_ref(_layernorm(x, axis=-1), ctx_1024, ctx_1024, mask_SxS2_bk1, L0_xattn_Wq, L0_xattn_Wk, L0_xattn_Wv, L0_xattn_wq_h, L0_xattn_bq_h, L0_xattn_wk_h, L0_xattn_bk_h, L0_xattn_wv_h, L0_xattn_bv_h, L0_xattn_Wo)
    x = x + _L0_ffn_ref(_layernorm(x, axis=-1), L0_ffn_w1, L0_ffn_b1, L0_ffn_w2, L0_ffn_b2)
    return x

_drawn_inputs = setup_inputs


def setup_inputs(seed=0):
    import zlib

    import numpy as np

    out = dict(_drawn_inputs(seed))
    spreads = {}
    factors = {'L0_xattn_bq_h': 3.185, 'L0_xattn_bk_h': 8.0, 'L0_ffn_b1': 8.0, 'L0_ffn_b2': 3.518}
    for name, (base, spread) in spreads.items():
        noise = np.random.default_rng([zlib.crc32(name.encode()), seed]).standard_normal(out[name].shape)
        drawn = base * np.exp(spread * noise) if base else spread * noise
        out[name] = jnp.asarray(drawn.astype(out[name].dtype))
    for name, factor in factors.items():
        out[name] = (out[name] * factor).astype(out[name].dtype)
    return out
```

```python
from contextlib import ExitStack

import concourse.bass as bass
from concourse import mybir

ALU = mybir.AluOpType
ACT = mybir.ActivationFunctionType
AX = mybir.AxisListType
F32 = mybir.dt.float32
F16 = mybir.dt.float16
U32 = mybir.dt.uint32
U8 = mybir.dt.uint8

P = 128
EPS = 1e-5
MASKED = -1000000000.0
X_SCALE = 2048.0
H_TOP = 2.0 ** 14
LEAST_BOUND = 1e-20


def xattn_ffn_kernel(nc, x, ctx_in, mask, Wq, Wk, Wv, wq_h, bq_h, wk_h, bk_h, wv_h, bv_h, Wo,
                     w1, b1, w2, b2, out):
    B, S, D = x.shape
    SK = ctx_in.shape[1]
    HD = wq_h.shape[1]
    H = w1.shape[0]
    T = S // P
    KD = D // P
    C = H // P
    KT = B * SK // P
    HALF = 512
    NH = B * SK // HALF
    SCORE_SCALE = float(HD) ** -0.5
    assert S == 512 and D == 256 and SK == 64 and HD == 16 and C == 8 and B % 2 == 0 and NH == 2

    x_v = x.rearrange("b (p j) d -> b p j d", p=P)
    out_v = out.rearrange("b (p j) d -> b p j d", p=P)

    with ExitStack() as stack:
        def sb(name, shape, dt=F32):
            return stack.enter_context(nc.sbuf_tensor(name, shape, dt))

        def sem(name):
            return stack.enter_context(nc.semaphore(name))

        ident = sb("ident", [P, P])
        ident16 = sb("ident16", [P, P], F16)
        ones = sb("ones", [P, P])
        sel = sb("sel", [P, HD])
        wq_sb = sb("wq_sb", [P, KD, D])
        wk_sb = sb("wk_sb", [P, KD, D])
        wv_sb = sb("wv_sb", [P, KD, D])
        wo_sb = sb("wo_sb", [P, KD, D])
        wqT = sb("wqT", [P, KD, D])
        wkT = sb("wkT", [P, KD, D])
        wvT = sb("wvT", [P, KD, D])
        qh_sb = sb("qh_sb", [P, KD, HD])
        kh_sb = sb("kh_sb", [P, KD, HD])
        vh_sb = sb("vh_sb", [P, KD, HD])
        bq_col = sb("bq_col", [HD, 1])
        bk_col = sb("bk_col", [HD, 1])
        bv_col = sb("bv_col", [HD, 1])
        bq_rep = sb("bq_rep", [HD, P])
        ctx_sb = sb("ctx_sb", [P, KT, D])
        ctxT = sb("ctxT", [P, KD, B * SK])
        wqhT = sb("wqhT", [HD, D])
        wkvh = sb("wkvh", [P, 2 * KD, HD])
        wo_sum = sb("wo_sum", [HD, D])
        khT = sb("khT", [HD, B * SK])
        vhT = sb("vhT", [HD, B, 2, SK])
        M_sb = sb("M_sb", [P, KD, B * SK])
        c_sb = sb("c_sb", [P, B * SK])
        V_sb = sb("V_sb", [P, B, 2 * D])
        mask_sb = sb("mask_sb", [P, T, SK], U8)
        masked_sb = sb("masked_sb", [P, T, SK])
        w1_sb = sb("w1_sb", [P, C, D])
        w2_sb = sb("w2_sb", [P, KD, H])
        neg1 = sb("neg1", [P, C * D], F16)
        neg2 = sb("neg2", [P, KD * H], F16)
        sgn1 = sb("sgn1", [P, C * D], F16)
        sgn2 = sb("sgn2", [P, KD * H], F16)
        sgn1T = sb("sgn1T", [P, KD, H], F16)
        sgn2T = sb("sgn2T", [P, C, D], F16)
        b1_col = sb("b1_col", [P, C])
        b1_row = sb("b1_row", [C, P])
        b2_bc = sb("b2_bc", [P, D])
        abs1 = sb("abs1", [P, C])
        alpha1x = sb("alpha1x", [P, C])
        bound = sb("bound", [P, C])
        b1_abs = sb("b1_abs", [P, C])
        top = sb("top", [P, 1])
        top_all = sb("top_all", [P, 1])
        pow2 = sb("pow2", [P, 1])
        inv_pow2 = sb("inv_pow2", [P, 1])
        h_scale = sb("h_scale", [P, 1])
        h_unscale = sb("h_unscale", [P, 1])
        abs2 = sb("abs2", [P, KD])
        diag2 = sb("diag2", [P, KD, P])
        alpha2_bc = sb("alpha2_bc", [P, D])
        mhalf = sb("mhalf", [P, T])

        x_in = [sb(f"x_in{n}", [P, T, D]) for n in range(2)]
        st_raw = [sb(f"st_raw{n}", [P, T, 6]) for n in range(2)]
        st = [sb(f"st{n}", [P, T, 2]) for n in range(2)]
        nmean = [sb(f"nmean{n}", [P, T]) for n in range(2)]
        vare = [sb(f"vare{n}", [P, T]) for n in range(2)]
        rstd = [sb(f"rstd{n}", [P, T]) for n in range(2)]
        nmr = [sb(f"nmr{n}", [P, T]) for n in range(2)]
        xh = [sb(f"xh{n}", [P, T, D]) for n in range(2)]
        xT1 = sb("xT1", [P, KD, S])
        sc = sb("sc", [P, T, SK])
        nmax = sb("nmax", [P, T])
        e_sb = sb("e_sb", [P, T, SK])
        esum = sb("esum", [P, T])
        einv = sb("einv", [P, T])
        eT = sb("eT", [P, T // 2, P])
        x1 = [sb(f"x1_{n}", [P, T, D]) for n in range(2)]
        x_hi = [sb(f"x_hi{n}", [P, KD, S], F16) for n in range(2)]
        x_lo = [sb(f"x_lo{n}", [P, KD, S], F16) for n in range(2)]
        h_sb = [sb(f"h_sb{n}", [P, S]) for n in range(2)]
        h_hi = [sb(f"h_hi{n}", [P, S], F16) for n in range(4)]
        h_lo = [sb(f"h_lo{n}", [P, S], F16) for n in range(4)]
        z_sb = [sb(f"z_sb{n}", [P, T, D]) for n in range(2)]

        psY = [stack.enter_context(nc.psum_tensor(f"psY{n}", [P, 512], F32)) for n in range(3)]
        psZ = [stack.enter_context(nc.psum_tensor(f"psZ{n}", [P, 512], F32)) for n in range(2)]
        psW = [stack.enter_context(nc.psum_tensor(f"psW{n}", [P, 512], F32)) for n in range(2)]
        psC = stack.enter_context(nc.psum_tensor("psC", [P, 512], F32))

        loaded = {n: sem("ld_" + n) for n in
                  ("wq", "wk", "wv", "wo", "heads", "ctx", "mask", "w1", "w2", "b1", "b2")}
        consts = sem("consts")
        identity = sem("identity")
        sel_ready = sem("sel_ready")
        bq_ready = sem("bq_ready")
        pe_wT = sem("pe_wT")
        pe_ctxT = sem("pe_ctxT")
        pe_heads = sem("pe_heads")
        pe_khT = sem("pe_khT")
        pe_vhT = sem("pe_vhT")
        pe_M = sem("pe_M")
        pe_V = sem("pe_V")
        pe_b1 = sem("pe_b1")
        pe_sgn = sem("pe_sgn")
        pe_alpha2 = sem("pe_alpha2")
        wT_copied = sem("wT_copied")
        ctxT_copied = sem("ctxT_copied")
        heads_copied = sem("heads_copied")
        khT_copied = sem("khT_copied")
        vhT_copied = sem("vhT_copied")
        M_copied = sem("M_copied")
        V_copied = sem("V_copied")
        V_zeroed = sem("V_zeroed")
        b1_copied = sem("b1_copied")
        sgn_steps = sem("sgn_steps")
        sgn1_ready = sem("sgn1_ready")
        sgn2_ready = sem("sgn2_ready")
        sgnT_copied = sem("sgnT_copied")
        top_ready = sem("top_ready")
        top_reduced = sem("top_reduced")
        scale_steps = sem("scale_steps")
        alpha1_ready = sem("alpha1_ready")
        scales_ready = sem("scales_ready")
        diag2_ready = sem("diag2_ready")
        alpha2_ready = sem("alpha2_ready")

        x_loaded = [sem(f"x_loaded{n}") for n in range(2)]
        out_stored = [sem(f"out_stored{n}") for n in range(2)]
        raw_stats = [sem(f"raw_stats{n}") for n in range(2)]
        stats = [sem(f"stats{n}") for n in range(2)]
        norm_steps = [sem(f"norm_steps{n}") for n in range(2)]
        normed = [sem(f"normed{n}") for n in range(2)]
        x_turned = sem("x_turned")
        xT1_copied = sem("xT1_copied")
        scored = sem("scored")
        sc_steps = sem("sc_steps")
        sc_maxed = sem("sc_maxed")
        exped = sem("exped")
        einv_ready = sem("einv_ready")
        e_turned = sem("e_turned")
        eT_copied = sem("eT_copied")
        attended = sem("attended")
        x1_ready = sem("x1_ready")
        x1_turned = sem("x1_turned")
        hi_copied = sem("hi_copied")
        lo_copied = sem("lo_copied")
        y_ready = sem("y_ready")
        gelu_done = sem("gelu_done")
        h_hi_done = sem("h_hi_done")
        h_lo_done = sem("h_lo_done")
        z_added = sem("z_added")
        z_scaled = sem("z_scaled")
        x1b_ready = sem("x1b_ready")
        out_ready = sem("out_ready")

        wait_carrier = sem("wait_carrier")

        block = stack.enter_context(nc.Block())

        def val(i, par, per, n):
            return i * (2 * per) + (per * par + n)

        def dma_val(i, par):
            return i * 16 + 16 * (par // 2 + 1)

        def wait(eng, s, v):
            if not isinstance(v, int) or v > 0:
                eng.wait_ge(s, v)

        def wait_apart(eng, s, v):
            if not isinstance(v, int) or v > 0:
                eng.wait_ge(s, v)
                eng.sem_inc(wait_carrier, 1)

        def has(i, par):
            return not isinstance(i, int) or 0 <= 2 * i + par < B

        def pipeline(eng, body, ahead=2):
            pairs = (B - ahead) // 2
            for b in range(-2, 2):
                body(b // 2, b % 2)
            with eng.Fori(1, pairs) as i:
                body(i, 0)
                body(i, 1)
            for b in range(2 * pairs, B + 1):
                body(b // 2, b % 2)

        @block.sync
        def _(sp):
            def rows(w):
                return w.rearrange("(k p) n -> p k n", p=P)

            def col(v):
                return v.rearrange("(p a) -> p a", a=1)

            def load_x(i, par):
                sp.dma_start(x_in[par % 2][:, :, :], x_v[i * 2 + par, :, :, :]) \
                  .then_inc(x_loaded[par % 2], 16)

            sp.dma_start(wk_sb[:, :, :], rows(Wk)).then_inc(loaded["wk"], 16)
            sp.dma_start(wq_sb[:, :, :], rows(Wq)).then_inc(loaded["wq"], 16)
            sp.dma_start(ctx_sb[:, :, :], ctx_in.rearrange("b t d -> (b t) d")
                         .rearrange("(n p) d -> p n d", p=P)).then_inc(loaded["ctx"], 16)
            load_x(0, 0)
            sp.dma_start(wv_sb[:, :, :], rows(Wv)).then_inc(loaded["wv"], 16)
            sp.dma_start(wo_sb[:, :, :], rows(Wo)).then_inc(loaded["wo"], 16)
            load_x(0, 1)
            sp.dma_start(w1_sb[:, :, :], rows(w1)).then_inc(loaded["w1"], 16)
            sp.dma_start(w2_sb[:, :, :], rows(w2)).then_inc(loaded["w2"], 16)

            def body(i, par):
                if has(i, par + 3) and not (isinstance(i, int) and 2 * i + par == -2):
                    wait(sp, x1_ready, val(i, par + 1, 1, 1))
                    load_x(i, par + 3)
                if has(i, par - 1):
                    wait(sp, out_ready, val(i, par - 1, 1, 1))
                    sp.dma_start(out_v[i * 2 + (par - 1), :, :, :], z_sb[(par - 1) % 2][:, :, :]) \
                      .then_inc(out_stored[(par - 1) % 2], 16)

            pipeline(sp, body, ahead=3)
            for s in out_stored:
                sp.wait_ge(s, 16 * (B // 2))

        @block.gpsimd
        def _(pool):
            nc.gpsimd.memset(ident[:, :], 0.0).then_inc(consts, 1)
            nc.gpsimd.memset(ident16[:, :], 0.0).then_inc(consts, 1)
            nc.gpsimd.memset(ones[:, :], 1.0).then_inc(consts, 1)
            nc.gpsimd.memset(mhalf[:, :], -0.5).then_inc(consts, 1)
            nc.gpsimd.memset(masked_sb[:, :, :], MASKED).then_inc(consts, 1)
            pool.wait_ge(consts, 2)
            for m in (ident, ident16):
                nc.gpsimd.affine_select(out=m[:, :], in_=m[:, :], compare_op=ALU.not_equal,
                                        fill=1.0, base=0, pattern=[[-1, P]],
                                        channel_multiplier=1).then_inc(identity, 1)
            pool.wait_ge(consts, 5)
            pool.wait_ge(identity, 2)
            nc.gpsimd.memset(V_sb[0:SK, :, D:], 0.0).then_inc(V_zeroed, 1)
            pool.wait_ge(V_zeroed, 1)
            nc.gpsimd.memset(V_sb[SK:, :, 0:D], 0.0).then_inc(V_zeroed, 1)
            pool.wait_ge(V_zeroed, 2)

            def norm(i, par, n, src, src_ready):
                wait_apart(pool, stats[n], val(i, par, 1, 1))
                nc.gpsimd.tensor_scalar(vare[n][:, :], st[n][:, :, 1], 1.0, EPS, ALU.mult, ALU.add) \
                    .then_inc(norm_steps[n], 1)
                nc.gpsimd.tensor_scalar(nmean[n][:, :], st[n][:, :, 0], -1.0, 1.0, ALU.mult,
                                        ALU.mult).then_inc(norm_steps[n], 1)
                wait(pool, norm_steps[n], val(i, par, 4, 2))
                nc.gpsimd.tensor_tensor(rstd[n][:, :], vare[n][:, :], mhalf[:, :], ALU.pow) \
                    .then_inc(norm_steps[n], 1)
                wait(pool, norm_steps[n], val(i, par, 4, 3))
                nc.gpsimd.tensor_tensor(nmr[n][:, :], nmean[n][:, :], rstd[n][:, :], ALU.mult) \
                    .then_inc(norm_steps[n], 1)
                wait(pool, (x_turned, x1_turned)[n], val(i, par - 1, KD, KD))
                wait_apart(pool, norm_steps[n], val(i, par, 4, 4))
                for j in range(T):
                    last = nc.gpsimd.tensor_scalar(xh[n][:, j, :], src[:, j, :],
                                                   rstd[n][:, j:j + 1], nmr[n][:, j:j + 1],
                                                   ALU.mult, ALU.add)
                last.then_inc(normed[n], 1)

            def top_of_hidden():
                pool.wait_ge(top_ready, 1)
                nc.gpsimd.partition_all_reduce(top_all[:, :], top[:, :], P,
                                               bass.bass_isa.ReduceOp.max).then_inc(top_reduced, 1)

            def body(i, par):
                if has(i, par + 2):
                    norm(i, par + 2, 0, x_in[par % 2], None)
                if has(i, par - 1):
                    n = (par - 1) % 2
                    wait(pool, z_scaled, val(i, par - 1, 2, 2))
                    wait(pool, x1b_ready, val(i, par - 1, 1, 1))
                    nc.gpsimd.tensor_tensor(z_sb[n][:, :, :], z_sb[n][:, :, :], x1[n][:, :, :],
                                            ALU.add).then_inc(out_ready, 1)
                if has(i, par + 1):
                    n = (par + 1) % 2
                    norm(i, par + 1, 1, x1[n], None)
                    wait(pool, normed[1], val(i, par + 1, 1, 1))
                    for j in range(T):
                        last = nc.gpsimd.tensor_tensor(x1[n][:, j, :], x1[n][:, j, :], b2_bc[:, :],
                                                       ALU.add)
                    last.then_inc(x1b_ready, 1)
                if isinstance(i, int) and 2 * i + par == -2:
                    top_of_hidden()
                    pool.wait_ge(loaded["b2"], 16)

            pipeline(pool, body)

        @block.scalar
        def _(act):
            act.dma_start(qh_sb[:, :, :], wq_h.rearrange("(k p) h -> p k h", p=P)).then_inc(loaded["heads"], 16)
            act.dma_start(kh_sb[:, :, :], wk_h.rearrange("(k p) h -> p k h", p=P)).then_inc(loaded["heads"], 16)
            act.dma_start(vh_sb[:, :, :], wv_h.rearrange("(k p) h -> p k h", p=P)).then_inc(loaded["heads"], 16)
            for dst, src in ((bq_col, bq_h), (bk_col, bk_h), (bv_col, bv_h)):
                act.dma_start(dst[:, :], src.rearrange("(p a) -> p a", a=1)).then_inc(loaded["heads"], 16)
            act.dma_start(b1_row[:, :], b1.rearrange("(c p) -> c p", p=P)).then_inc(loaded["b1"], 16)
            act.dma_start(mask_sb[:, :, :], mask.rearrange("(p j) t -> p j t", p=P)).then_inc(loaded["mask"], 16)
            act.dma_start(b2_bc[:, :], b2.rearrange("(a n) -> a n", a=1).to_broadcast([P, D])).then_inc(loaded["b2"], 16)

            for n, w in enumerate((wkT, wqT, wvT)):
                act.wait_ge(pe_wT, n + 1)
                nc.scalar.activation(w[:, :, :].rearrange("p k n -> p (k n)"), psY[n][:, :],
                                     ACT.Copy).then_inc(wT_copied, 1)
            for k in range(KD):
                for n in range(NH):
                    act.wait_ge(pe_M, k * NH + n + 1)
                    nc.scalar.activation(M_sb[:, k, n * HALF:(n + 1) * HALF],
                                         (psW[0], psW[1], psC, psY[0])[k * NH + n][:, :],
                                         ACT.Copy).then_inc(M_copied, 1)
            for n in range(B // 2):
                act.wait_ge(pe_V, n + 1)
                act.wait_ge(V_zeroed, 2)
                for h in range(2):
                    rows = slice(h * SK, (h + 1) * SK)
                    nc.scalar.activation(V_sb[rows, 2 * n:2 * n + 2, h * D:(h + 1) * D],
                                         psZ[n % 2][rows, :].rearrange("p (b d) -> p b d", b=2),
                                         ACT.Copy).then_inc(V_copied, 1)

            def exp(i, par):
                wait(act, sc_maxed, val(i, par, 1, 1))
                wait(act, e_turned, val(i, par - 1, 1, 1))
                wait(act, einv_ready, val(i, par - 1, 1, 1))
                for j in range(T):
                    last = nc.scalar.activation(e_sb[:, j, :], sc[:, j, :], ACT.Exp,
                                                bias=nmax[:, j:j + 1], scale=1.0,
                                                accum_out=esum[:, j:j + 1])
                last.then_inc(exped, 1)

            def gelu(i, par, c):
                wait(act, y_ready, val(i, par, C, c + 1))
                wait(act, h_lo_done, val(i, par, C, c - 1))
                nc.scalar.activation(h_sb[c % 2][:, :], psY[c % 3][:, :], ACT.Gelu,
                                     bias=b1_col[:, c:c + 1], scale=alpha1x[:, c:c + 1]) \
                    .then_inc(gelu_done, 1)

            def body(i, par):
                late, early, ffn = has(i, par + 1), has(i, par + 2), has(i, par)
                if late:
                    exp(i, par + 1)
                if ffn:
                    if isinstance(i, int) and 2 * i + par == 0:
                        act.wait_ge(alpha1_ready, 1)
                        act.wait_ge(b1_copied, 1)
                    gelu(i, par, 0)
                    gelu(i, par, 1)
                if late:
                    wait(act, e_turned, val(i, par + 1, 1, 1))
                    wait(act, attended, val(i, par, 2, 2))
                    nc.scalar.activation(eT[:, :, :].rearrange("p n t -> p (n t)"),
                                         psC[:, 0:T // 2 * P], ACT.Copy).then_inc(eT_copied, 1)
                if ffn:
                    for c in (2, 3, 4):
                        gelu(i, par, c)
                if early:
                    wait(act, scored, val(i, par + 1, 1, 1))
                    for k in range(KD):
                        wait(act, x_turned, val(i, par + 2, KD, k + 1))
                        nc.scalar.activation(xT1[:, k, :], psW[k][:, :], ACT.Copy).then_inc(xT1_copied, 1)
                if ffn:
                    gelu(i, par, 5)
                    gelu(i, par, 6)
                if late:
                    n = (par + 1) % 2
                    wait(act, y_ready, val(i, par - 1, C, C))
                    for k in range(KD):
                        wait(act, x1_turned, val(i, par + 1, KD, k + 1))
                        nc.scalar.activation(x_hi[n][:, k, :], psW[k][:, :], ACT.Copy,
                                             scale=X_SCALE).then_inc(hi_copied, 1)
                if ffn:
                    gelu(i, par, 7)

            pipeline(act, body)

        @block.vector
        def _(dve):
            dve.wait_ge(identity, 1)
            nc.vector.tensor_reduce(sel[:, :], ident[:, :].rearrange("p (g h) -> p h g", h=HD),
                                    AX.X, ALU.add).then_inc(sel_ready, 1)
            dve.wait_ge(loaded["heads"], 96)
            dve.wait_ge(consts, 5)
            nc.vector.tensor_scalar(bq_rep[:, :], ones[0:HD, :], bq_col[:, :], None,
                                    ALU.mult).then_inc(bq_ready, 1)
            for k in range(KD):
                for n in range(NH):
                    m = k * NH + n
                    dve.wait_ge(pe_ctxT, m + 1)
                    nc.vector.tensor_copy(ctxT[:, k, n * HALF:(n + 1) * HALF],
                                          (psZ[0], psZ[1], psW[0], psW[1])[m][:, :]) \
                        .then_inc(ctxT_copied, 1)
            dve.wait_ge(pe_heads, 1)
            nc.vector.tensor_copy(wkvh[:, :, :].rearrange("p k h -> p (k h)"),
                                  psC[:, D:D + 2 * KD * HD]).then_inc(heads_copied, 1)
            nc.vector.tensor_copy(wqhT[:, :], psC[0:HD, 0:D]).then_inc(heads_copied, 1)
            for n in range(NH):
                dve.wait_ge(pe_khT, n + 1)
                nc.vector.tensor_scalar(khT[:, n * HALF:(n + 1) * HALF], psY[1 + n][0:HD, :],
                                        bk_col[:, :], SCORE_SCALE, ALU.add, ALU.mult) \
                    .then_inc(khT_copied, 1)
            for n in range(NH):
                dve.wait_ge(pe_vhT, n + 1)
                for h in range(2):
                    nc.vector.tensor_scalar(vhT[:, n * (B // 2):(n + 1) * (B // 2), h, :],
                                            psZ[n][0:HD, :].rearrange("p (b t) -> p b t", t=SK),
                                            bv_col[:, :], None, ALU.add).then_inc(vhT_copied, 1)
            dve.wait_ge(pe_vhT, 3)
            nc.vector.tensor_copy(wo_sum[:, :], psY[0][0:HD, 0:D]).then_inc(vhT_copied, 1)

            def raw_bn(n, src):
                for j in range(T):
                    last = nc.vector.bn_stats(st_raw[n][:, j, :], src[:, j, :])
                return last

            def bn(i, par, n):
                wait(dve, normed[n], val(i, par - 1, 1, 1))
                wait_apart(dve, raw_stats[n], val(i, par, 1, 1))
                for j in range(T):
                    last = nc.vector.bn_aggr(st[n][:, j, :], st_raw[n][:, j, :])
                last.then_inc(stats[n], 1)

            def split(i, par, c):
                wait(dve, gelu_done, val(i, par, C, c + 1))
                wait(dve, z_added, val(i, par, C, c - 3))
                nc.vector.tensor_scalar(h_hi[c % 4][:, :], h_sb[c % 2][:, :], h_scale[:, :], None,
                                        ALU.mult).then_inc(h_hi_done, 1)
                wait(dve, h_hi_done, val(i, par, C, c + 1))
                nc.vector.scalar_tensor_tensor(out=h_lo[c % 4][:, :], in0=h_sb[c % 2][:, :],
                                               scalar=h_scale[:, :], in1=h_hi[c % 4][:, :],
                                               op0=ALU.mult, op1=ALU.subtract).then_inc(h_lo_done, 1)

            def scores(i, par):
                wait(dve, scored, val(i, par, 1, 1))
                wait(dve, exped, val(i, par - 1, 1, 1))
                b0 = i * (2 * SK) + par * SK
                nc.vector.tensor_tensor(
                    sc[:, :, :], psC[:, 0:T * SK].rearrange("p (j t) -> p j t", j=T),
                    c_sb[:, bass.ds(b0, SK)].unsqueeze(1).to_broadcast([P, T, SK]), ALU.add) \
                    .then_inc(sc_steps, 1)
                wait_apart(dve, sc_steps, val(i, par, 2, 1))
                nc.vector.copy_predicated(sc[:, :, :], mask_sb[:, :, :], masked_sb[:, :, :]) \
                    .then_inc(sc_steps, 1)
                wait(dve, sc_steps, val(i, par, 2, 2))
                nc.vector.tensor_reduce(nmax[:, :], sc[:, :, :], AX.X, ALU.max, negate=True) \
                    .then_inc(sc_maxed, 1)

            def setup_weights():
                dve.wait_ge(loaded["w1"], 16)
                w1_f = w1_sb[:, :, :].rearrange("p c d -> p (c d)")
                nc.vector.tensor_scalar(neg1[:, :], w1_f, 0.0, None, ALU.is_lt).then_inc(sgn_steps, 1)
                nc.vector.tensor_reduce(abs1[:, :], w1_sb[:, :, :], AX.X, ALU.add,
                                        apply_absolute_value=True).then_inc(scale_steps, 1)
                dve.wait_ge(sgn_steps, 1)
                nc.vector.scalar_tensor_tensor(out=sgn1[:, :], in0=w1_f, scalar=0.0, in1=neg1[:, :],
                                               op0=ALU.is_gt, op1=ALU.subtract).then_inc(sgn1_ready, 1)
                dve.wait_ge(scale_steps, 1)
                nc.vector.tensor_scalar(alpha1x[:, :], abs1[:, :], 1.0 / (D * X_SCALE), None,
                                        ALU.mult).then_inc(alpha1_ready, 1)
                dve.wait_ge(b1_copied, 1)
                nc.vector.scalar_tensor_tensor(out=b1_abs[:, :], in0=b1_col[:, :], scalar=-1.0,
                                               in1=b1_col[:, :], op0=ALU.mult, op1=ALU.max) \
                    .then_inc(scale_steps, 1)
                dve.wait_ge(scale_steps, 2)
                nc.vector.scalar_tensor_tensor(out=bound[:, :], in0=abs1[:, :], scalar=1.001,
                                               in1=b1_abs[:, :], op0=ALU.mult, op1=ALU.add) \
                    .then_inc(scale_steps, 1)
                dve.wait_ge(scale_steps, 3)
                nc.vector.tensor_reduce(top[:, :], bound[:, :], AX.X, ALU.max).then_inc(top_ready, 1)
                dve.wait_ge(loaded["w2"], 16)
                w2_f = w2_sb[:, :, :].rearrange("p k n -> p (k n)")
                nc.vector.tensor_scalar(neg2[:, :], w2_f, 0.0, None, ALU.is_lt).then_inc(sgn_steps, 1)
                nc.vector.tensor_reduce(abs2[:, :], w2_sb[:, :, :], AX.X, ALU.add,
                                        apply_absolute_value=True).then_inc(scale_steps, 1)
                dve.wait_ge(sgn_steps, 2)
                nc.vector.scalar_tensor_tensor(out=sgn2[:, :], in0=w2_f, scalar=0.0, in1=neg2[:, :],
                                               op0=ALU.is_gt, op1=ALU.subtract).then_inc(sgn2_ready, 1)
                dve.wait_ge(scale_steps, 4)
                for k in range(KD):
                    nc.vector.tensor_scalar(diag2[:, k, :], ident[:, :], abs2[:, k:k + 1], 1.0 / H,
                                            ALU.mult, ALU.mult).then_inc(diag2_ready, 1)
                dve.wait_ge(top_reduced, 1)
                nc.vector.tensor_scalar(top[:, :], top_all[:, :], LEAST_BOUND, None, ALU.max) \
                    .then_inc(scale_steps, 1)
                dve.wait_ge(scale_steps, 5)
                nc.vector.tensor_scalar(pow2[:, :].bitcast(U32), top[:, :].bitcast(U32), 0x7F800000,
                                        None, ALU.bitwise_and).then_inc(scale_steps, 1)
                dve.wait_ge(scale_steps, 6)
                nc.vector.reciprocal(inv_pow2[:, :], pow2[:, :]).then_inc(scale_steps, 1)
                nc.vector.tensor_scalar(h_unscale[:, :], pow2[:, :], 1.0 / H_TOP, None,
                                        ALU.mult).then_inc(scale_steps, 1)
                dve.wait_ge(scale_steps, 8)
                nc.vector.tensor_scalar(h_scale[:, :], inv_pow2[:, :], H_TOP, None,
                                        ALU.mult).then_inc(scales_ready, 1)
                for n in range(4):
                    dve.wait_ge(pe_sgn, n + 1)
                    dst = (sgn1T[:, 0, :], sgn1T[:, 1, :],
                           sgn2T[:, 0:4, :].rearrange("p c d -> p (c d)"),
                           sgn2T[:, 4:8, :].rearrange("p c d -> p (c d)"))[n]
                    nc.vector.tensor_copy(dst, (psY[0], psY[1], psY[2], psZ[0])[n][:, :].bitcast(F16)) \
                        .then_inc(sgnT_copied, 1)
                dve.wait_ge(pe_alpha2, 1)
                nc.vector.tensor_scalar(alpha2_bc[:, :], psZ[1][:, 0:D], h_unscale[:, :], None,
                                        ALU.mult).then_inc(alpha2_ready, 1)
                dve.wait_ge(alpha2_ready, 1)
                dve.wait_ge(scales_ready, 1)

            def body(i, par):
                late, early, ffn, prev = (has(i, par + d) for d in (1, 2, 0, -1))
                first = isinstance(i, int) and 2 * i + par == -2
                if prev:
                    split(i, par - 1, C - 1)
                if early:
                    n = par % 2
                    wait(dve, x_loaded[n], dma_val(i, par + 2))
                    raw_bn(0, x_in[n]).then_inc(raw_stats[0], 1)
                    bn(i, par + 2, 0)
                if first:
                    for n in range(NH):
                        dve.wait_ge(pe_M, 5 + n)
                        nc.vector.tensor_copy(c_sb[:, n * HALF:(n + 1) * HALF], psY[1 + n][:, :]) \
                            .then_inc(M_copied, 1)
                    dve.wait_ge(pe_b1, 1)
                    nc.vector.tensor_copy(b1_col[:, :], psC[:, 0:C]).then_inc(b1_copied, 1)
                    dve.wait_ge(M_copied, 6)
                    dve.wait_ge(loaded["mask"], 16)
                if late:
                    wait(dve, exped, val(i, par + 1, 1, 1))
                    nc.vector.reciprocal(einv[:, :], esum[:, :]).then_inc(einv_ready, 1)
                if prev:
                    m = (par - 1) % 2
                    wait(dve, z_added, val(i, par - 1, C, C))
                    wait(dve, out_stored[m], dma_val(i, par - 3))
                    for n in range(2):
                        nc.vector.tensor_tensor(
                            z_sb[m][:, 2 * n:2 * n + 2, :],
                            psZ[n][:, :].rearrange("p (j d) -> p j d", j=2),
                            alpha2_bc[:, :].unsqueeze(1).to_broadcast([P, 2, D]), ALU.mult) \
                            .then_inc(z_scaled, 1)
                if ffn:
                    for c in range(4):
                        split(i, par, c)
                if late:
                    m = (par + 1) % 2
                    wait(dve, einv_ready, val(i, par + 1, 1, 1))
                    wait(dve, out_ready, val(i, par - 1, 1, 1))
                    for j in range(T):
                        if j % 2 == 0:
                            wait(dve, attended, val(i, par + 1, 2, j // 2 + 1))
                        last = nc.vector.scalar_tensor_tensor(
                            out=x1[m][:, j, :], in0=psW[j // 2][:, (j % 2) * D:(j % 2 + 1) * D],
                            scalar=einv[:, j:j + 1], in1=x_in[m][:, j, :], op0=ALU.mult, op1=ALU.add)
                    last.then_inc(x1_ready, 1)
                    wait(dve, x1_ready, val(i, par + 1, 1, 1))
                    raw_bn(1, x1[m]).then_inc(raw_stats[1], 1)
                    bn(i, par + 1, 1)
                if ffn:
                    split(i, par, 4)
                    split(i, par, 5)
                if early:
                    scores(i, par + 2)
                if first:
                    setup_weights()
                if ffn:
                    split(i, par, 6)
                if late:
                    m = (par + 1) % 2
                    for k in range(KD):
                        wait(dve, hi_copied, val(i, par + 1, KD, k + 1))
                        nc.vector.scalar_tensor_tensor(out=x_lo[m][:, k, :], in0=psW[k][:, :],
                                                       scalar=X_SCALE, in1=x_hi[m][:, k, :],
                                                       op0=ALU.mult, op1=ALU.subtract) \
                            .then_inc(lo_copied, 1)

            pipeline(dve, body)

        @block.tensor
        def _(pe):
            pe.wait_ge(identity, 2)
            pe.wait_ge(consts, 5)
            for n, (w, name) in enumerate(((wk_sb, "wk"), (wq_sb, "wq"), (wv_sb, "wv"))):
                if n == 2:
                    pe.wait_ge(loaded["ctx"], 16)
                    for k in range(KD):
                        for h in range(NH):
                            ps = (psZ[0], psZ[1], psW[0], psW[1])[k * NH + h]
                            for t in range(HALF // P):
                                last = nc.tensor.transpose(ps[:, t * P:(t + 1) * P],
                                                           ctx_sb[:, h * (HALF // P) + t, k * P:(k + 1) * P],
                                                           ident[:, :])
                            last.then_inc(pe_ctxT, 1)
                pe.wait_ge(loaded[name], 16)
                for k in range(KD):
                    for m in range(KD):
                        last = nc.tensor.transpose(psY[n][:, k * D + m * P:k * D + (m + 1) * P],
                                                   w[:, m, k * P:(k + 1) * P], ident[:, :])
                last.then_inc(pe_wT, 1)
            pe.wait_ge(loaded["heads"], 96)
            pe.wait_ge(wT_copied, 3)
            for k in range(KD):
                nc.tensor.matmul(psC[0:HD, 0:D], qh_sb[:, k, :], wqT[:, k, :], start=(k == 0), stop=(k == KD - 1))
            for n, (wT, hd) in enumerate(((wkT, kh_sb), (wvT, vh_sb))):
                for m in range(KD):
                    at = D + (n * KD + m) * HD
                    for k in range(KD):
                        last = nc.tensor.matmul(psC[:, at:at + HD], wT[:, k, m * P:(m + 1) * P],
                                                hd[:, k, :], start=(k == 0), stop=(k == KD - 1))
            last.then_inc(pe_heads, 1)
            pe.wait_ge(heads_copied, 2)
            pe.wait_ge(ctxT_copied, 4)
            for n in range(NH):
                for k in range(KD):
                    last = nc.tensor.matmul(psY[1 + n][0:HD, :], wkvh[:, k, :],
                                            ctxT[:, k, n * HALF:(n + 1) * HALF], start=(k == 0), stop=(k == KD - 1))
                last.then_inc(pe_khT, 1)
            for n in range(NH):
                for k in range(KD):
                    last = nc.tensor.matmul(psZ[n][0:HD, :], wkvh[:, KD + k, :],
                                            ctxT[:, k, n * HALF:(n + 1) * HALF], start=(k == 0), stop=(k == KD - 1))
                last.then_inc(pe_vhT, 1)
            pe.wait_ge(sel_ready, 1)
            pe.wait_ge(loaded["wo"], 16)
            for k in range(KD):
                last = nc.tensor.matmul(psY[0][0:HD, 0:D], sel[:, :], wo_sb[:, k, :], start=(k == 0), stop=(k == KD - 1))
            last.then_inc(pe_vhT, 1)
            pe.wait_ge(khT_copied, 2)
            pe.wait_ge(bq_ready, 1)
            pe.wait_ge(vhT_copied, 5)
            for k in range(KD):
                for n in range(NH):
                    nc.tensor.matmul((psW[0], psW[1], psC, psY[0])[k * NH + n][:, :],
                                     wqhT[:, k * P:(k + 1) * P], khT[:, n * HALF:(n + 1) * HALF],
                                     start=True, stop=True).then_inc(pe_M, 1)
            for n in range(NH):
                nc.tensor.matmul(psY[1 + n][:, :], bq_rep[:, :], khT[:, n * HALF:(n + 1) * HALF],
                                 start=True, stop=True).then_inc(pe_M, 1)
            for n in range(B // 2):
                if n >= 2:
                    pe.wait_ge(V_copied, 2 * (n - 1))
                for m in range(2):
                    b = 2 * n + m
                    last = nc.tensor.matmul(psZ[n % 2][:, m * D:(m + 1) * D],
                                            vhT[:, b, :, :].rearrange("p h t -> p (h t)"), wo_sum[:, :],
                                            start=True, stop=True)
                last.then_inc(pe_V, 1)
            pe.wait_ge(loaded["b1"], 16)
            pe.wait_ge(M_copied, 3)
            nc.tensor.transpose(psC[:, 0:C], b1_row[:, :], ident[0:C, 0:C]).then_inc(pe_b1, 1)

            def setup_signs():
                pe.wait_ge(sgn1_ready, 1)
                pe.wait_ge(M_copied, 6)
                for k in range(KD):
                    ps = psY[k][:, :].bitcast(F16)
                    for c in range(C):
                        last = nc.tensor.transpose(ps[:, c * P:(c + 1) * P],
                                                   sgn1[:, c * D + k * P:c * D + (k + 1) * P], ident16[:, :])
                    last.then_inc(pe_sgn, 1)
                pe.wait_ge(sgn2_ready, 1)
                pe.wait_ge(V_copied, B)
                for n in range(2):
                    ps = (psY[2], psZ[0])[n][:, :].bitcast(F16)
                    for c in range(4):
                        for k in range(KD):
                            a = k * H + (4 * n + c) * P
                            last = nc.tensor.transpose(ps[:, c * D + k * P:c * D + (k + 1) * P],
                                                       sgn2[:, a:a + P], ident16[:, :])
                    last.then_inc(pe_sgn, 1)
                pe.wait_ge(diag2_ready, 2)
                for k in range(KD):
                    last = nc.tensor.matmul(psZ[1][:, k * P:(k + 1) * P], ones[:, :], diag2[:, k, :],
                                            start=True, stop=True)
                last.then_inc(pe_alpha2, 1)

            def turn_x(i, par, n):
                wait(pe, normed[n], val(i, par, 1, 1))
                if n == 0:
                    wait(pe, lo_copied, val(i, par - 2, KD, KD))
                    wait(pe, x1_ready, val(i, par - 1, 1, 1))
                else:
                    wait(pe, xT1_copied, val(i, par + 1, KD, KD) if has(i, par + 1) else 0)
                    wait(pe, x1_ready, val(i, par, 1, 1))
                for k in range(KD):
                    for j in range(T):
                        last = nc.tensor.transpose(psW[k][:, j * P:(j + 1) * P],
                                                   xh[n][:, j, k * P:(k + 1) * P], ident[:, :])
                    last.then_inc((x_turned, x1_turned)[n], 1)

            def score(i, par):
                wait(pe, xT1_copied, val(i, par, KD, KD))
                wait(pe, eT_copied, val(i, par - 1, 1, 1))
                b0 = i * (2 * SK) + par * SK
                for j in range(T):
                    for k in range(KD):
                        last = nc.tensor.matmul(psC[:, j * SK:(j + 1) * SK], xT1[:, k, j * P:(j + 1) * P],
                                                M_sb[:, k, bass.ds(b0, SK)], start=(k == 0), stop=(k == KD - 1))
                last.then_inc(scored, 1)

            def turn_e(i, par):
                wait(pe, exped, val(i, par, 1, 1))
                for n in range(T // 2):
                    last = nc.tensor.transpose(psC[:, n * P:(n + 1) * P],
                                               e_sb[:, 2 * n:2 * n + 2, :].rearrange("p j t -> p (j t)"),
                                               ident[:, :])
                last.then_inc(e_turned, 1)

            def attend(i, par):
                wait(pe, eT_copied, val(i, par, 1, 1))
                wait(pe, lo_copied, val(i, par - 1, KD, KD))
                wait(pe, xT1_copied, val(i, par, KD, KD))
                for n in range(T // 2):
                    nc.tensor.matmul(psW[n][:, :], eT[:, n, :], V_sb[:, i * 2 + par, :],
                                     start=True, stop=True).then_inc(attended, 1)

            def first_product(i, par, c):
                if c == 0:
                    wait(pe, lo_copied, val(i, par, KD, KD))
                wait(pe, gelu_done, val(i, par, C, c - 1 if c < C % 3 else c - 2))
                slot = par % 2
                n = 0
                for k in range(KD):
                    for part in (x_hi, x_lo):
                        last = nc.tensor.matmul(psY[c % 3][:, :], sgn1T[:, k, c * P:(c + 1) * P],
                                                part[slot][:, k, :], start=(n == 0), stop=(n == 2 * KD - 1))
                        n += 1
                last.then_inc(y_ready, 1)

            def second_product(i, par, c):
                wait(pe, h_lo_done, val(i, par, C, c + 1))
                if c == 0:
                    wait(pe, z_scaled, val(i, par - 1, 2, 2))
                for j in range(T):
                    for n, part in enumerate((h_hi, h_lo)):
                        last = nc.tensor.matmul(psZ[j // 2][:, (j % 2) * D:(j % 2 + 1) * D],
                                                part[c % 4][:, j * P:(j + 1) * P], sgn2T[:, c, :],
                                                start=(c == 0 and n == 0 and j % 2 == 0),
                                                stop=(c == C - 1 and n == 1 and j % 2 == 1))
                last.then_inc(z_added, 1)

            def body(i, par):
                late, early, ffn, prev = (has(i, par + d) for d in (1, 2, 0, -1))
                if isinstance(i, int) and 2 * i + par == -1:
                    setup_signs()
                if isinstance(i, int) and 2 * i + par == 0:
                    pe.wait_ge(sgnT_copied, 4)
                    pe.wait_ge(alpha2_ready, 1)
                if ffn:
                    first_product(i, par, 0)
                if prev:
                    second_product(i, par - 1, 6)
                if ffn:
                    first_product(i, par, 1)
                if prev:
                    second_product(i, par - 1, 7)
                if late:
                    turn_e(i, par + 1)
                if ffn:
                    first_product(i, par, 2)
                    first_product(i, par, 3)
                    second_product(i, par, 0)
                if late:
                    attend(i, par + 1)
                if ffn:
                    second_product(i, par, 1)
                    first_product(i, par, 4)
                    second_product(i, par, 2)
                if early:
                    if isinstance(i, int) and 2 * i + par == -2:
                        pe.wait_ge(M_copied, 6)
                        pe.wait_ge(b1_copied, 1)
                    turn_x(i, par + 2, 0)
                if ffn:
                    first_product(i, par, 5)
                    second_product(i, par, 3)
                if early:
                    score(i, par + 2)
                if ffn:
                    first_product(i, par, 6)
                if late:
                    turn_x(i, par + 1, 1)
                if ffn:
                    second_product(i, par, 4)
                    first_product(i, par, 7)
                    second_product(i, par, 5)

            pipeline(pe, body)


_INS = ['x', 'ctx_1024', 'mask_SxS2_bk1', 'L0_xattn_Wq', 'L0_xattn_Wk', 'L0_xattn_Wv', 'L0_xattn_wq_h',
        'L0_xattn_bq_h', 'L0_xattn_wk_h', 'L0_xattn_bk_h', 'L0_xattn_wv_h', 'L0_xattn_bv_h',
        'L0_xattn_Wo', 'L0_ffn_w1', 'L0_ffn_b1', 'L0_ffn_w2', 'L0_ffn_b2']


def kernel(**inputs):
    import numpy as _np
    import concourse.bacc as _bacc
    from concourse import mybir as _mybir
    from concourse.bass_utils import run_bass_kernel_spmd as _run

    nc = _bacc.Bacc("TRN2", target_bir_lowering=False, num_devices=1)
    arrays, args = {}, []
    for name in _INS:
        a = _np.ascontiguousarray(inputs[name])
        arrays[f"in_{name}"] = a
        args.append(nc.dram_tensor(f"in_{name}", a.shape, _mybir.dt.from_np(a.dtype), kind="ExternalInput").ap())
    out = nc.dram_tensor("out_x", arrays["in_x"].shape, _mybir.dt.float32, kind="ExternalOutput").ap()
    xattn_ffn_kernel(nc, *args, out)
    r = _run(nc, [arrays], core_ids=[0])
    return r.results[0]["out_x"]
```

```python
from contextlib import ExitStack

import concourse.bass as bass
from concourse import mybir

ALU = mybir.AluOpType
ACT = mybir.ActivationFunctionType
AX = mybir.AxisListType
F32 = mybir.dt.float32
F16 = mybir.dt.float16
BF16 = mybir.dt.bfloat16
U32 = mybir.dt.uint32
U8 = mybir.dt.uint8

P = 128
EPS = 1e-5
MASKED = -1000000000.0
X_SCALE = 2048.0
H_TOP = 2.0 ** 14
LEAST_BOUND = 1e-20


def xattn_ffn_kernel(nc, x, ctx_in, mask, Wq, Wk, Wv, wq_h, bq_h, wk_h, bk_h, wv_h, bv_h, Wo,
                     w1, b1, w2, b2, out):
    B, S, D = x.shape
    SK = ctx_in.shape[1]
    HD = wq_h.shape[1]
    H = w1.shape[0]
    T = S // P
    KD = D // P
    C = H // P
    KT = B * SK // P
    HALF = 512
    NH = B * SK // HALF
    SCORE_SCALE = float(HD) ** -0.5
    V_AT = 32
    POOL_HI = (0, 5, 6, 7)
    ACT_HI = (1, 2, 3, 4)
    assert S == 512 and D == 256 and SK == 64 and HD == 16 and C == 8 and B % 2 == 0 and NH == 2

    x_v = x.rearrange("b (p j) d -> b p j d", p=P)
    out_v = out.rearrange("b (p j) d -> b p j d", p=P)

    with ExitStack() as stack:
        def sb(name, shape, dt=F32):
            return stack.enter_context(nc.sbuf_tensor(name, shape, dt))

        def sem(name):
            return stack.enter_context(nc.semaphore(name))

        ident = sb("ident", [P, P])
        ident16 = sb("ident16", [P, P], F16)
        ones = sb("ones", [P, P])
        sel = sb("sel", [P, V_AT + HD])
        wq_sb = sb("wq_sb", [P, KD, D])
        wk_sb = sb("wk_sb", [P, KD, D])
        wv_sb = sb("wv_sb", [P, KD, D])
        wo_sb = sb("wo_sb", [P, KD, D])
        wqT = sb("wqT", [P, KD, D])
        wkT = sb("wkT", [P, KD, D])
        wvT = sb("wvT", [P, KD, D])
        qh_sb = sb("qh_sb", [P, KD, HD])
        kh_sb = sb("kh_sb", [P, KD, HD])
        vh_sb = sb("vh_sb", [P, KD, HD])
        bq_col = sb("bq_col", [HD, 1])
        bk_col = sb("bk_col", [HD, 1])
        bv_col = sb("bv_col", [V_AT + HD, 1])
        bq_rep = sb("bq_rep", [HD, P])
        ctx_sb = sb("ctx_sb", [P, KT, D])
        ctxT = sb("ctxT", [P, KD, B * SK])
        wqhT = sb("wqhT", [HD, D])
        wkvh = sb("wkvh", [P, KD, V_AT + HD])
        wo_sum = sb("wo_sum", [V_AT + HD, D])
        khT = sb("khT", [HD, B * SK])
        vhT = sb("vhT", [V_AT + HD, B, 2, SK])
        M_sb = sb("M_sb", [P, KD, B * SK])
        c_sb = sb("c_sb", [P, B * SK])
        V_sb = sb("V_sb", [P, B, 2 * D])
        mask_sb = sb("mask_sb", [P, T, SK], U8)
        masked_sb = sb("masked_sb", [P, T, SK])
        w1_sb = sb("w1_sb", [P, C, D])
        w2_sb = sb("w2_sb", [P, KD, H])
        neg1 = sb("neg1", [P, C * D], F16)
        neg2 = sb("neg2", [P, KD * H], F16)
        sgn1 = sb("sgn1", [P, C * D], F16)
        sgn2 = sb("sgn2", [P, KD * H], F16)
        sgn1T = sb("sgn1T", [P, KD, H], F16)
        sgn2T = sb("sgn2T", [P, C, D], F16)
        b1_col = sb("b1_col", [P, C])
        b1_row = sb("b1_row", [C, P])
        b2_bc = sb("b2_bc", [P, D])
        abs1 = sb("abs1", [P, C])
        alpha1x = sb("alpha1x", [P, C])
        bound = sb("bound", [P, C])
        b1_abs = sb("b1_abs", [P, C])
        top = sb("top", [P, 1])
        top_all = sb("top_all", [P, 1])
        pow2 = sb("pow2", [P, 1])
        inv_pow2 = sb("inv_pow2", [P, 1])
        h_scale = sb("h_scale", [P, 1])
        h_unscale = sb("h_unscale", [P, 1])
        abs2 = sb("abs2", [P, KD])
        diag2 = sb("diag2", [P, KD, P])
        alpha2_bc = sb("alpha2_bc", [P, D])
        mhalf = sb("mhalf", [P, T])
        magnitudes = sb("magnitudes", [P, C * D], BF16)

        x_in = [sb(f"x_in{n}", [P, T, D]) for n in range(2)]
        st_raw = [sb(f"st_raw{n}", [P, T, 6]) for n in range(2)]
        st = [sb(f"st{n}", [P, T, 2]) for n in range(2)]
        nmean = [sb(f"nmean{n}", [P, T]) for n in range(2)]
        vare = [sb(f"vare{n}", [P, T]) for n in range(2)]
        rstd = [sb(f"rstd{n}", [P, T]) for n in range(2)]
        nmr = [sb(f"nmr{n}", [P, T]) for n in range(2)]
        xh = [sb(f"xh{n}", [P, T, D]) for n in range(2)]
        xT1 = sb("xT1", [P, KD, S])
        sc = sb("sc", [P, T, SK])
        nmax = sb("nmax", [P, T])
        e_sb = sb("e_sb", [P, T, SK])
        esum = sb("esum", [P, T])
        einv = sb("einv", [P, T])
        eT = sb("eT", [P, T // 2, P])
        x1 = sb("x1", [P, T, D])
        x1b = [sb(f"x1b{n}", [P, T, D]) for n in range(2)]
        x_hi = [sb(f"x_hi{n}", [P, KD, S], F16) for n in range(2)]
        x_lo = [sb(f"x_lo{n}", [P, KD, S], F16) for n in range(2)]
        h_sb = [sb(f"h_sb{n}", [P, S]) for n in range(4)]
        h_hi = [sb(f"h_hi{n}", [P, S], F16) for n in range(4)]
        h_lo = [sb(f"h_lo{n}", [P, S], F16) for n in range(4)]
        z_sb = [sb(f"z_sb{n}", [P, T, D]) for n in range(2)]

        psY = [stack.enter_context(nc.psum_tensor(f"psY{n}", [P, 512], F32)) for n in range(4)]
        psZ = [stack.enter_context(nc.psum_tensor(f"psZ{n}", [P, 512], F32)) for n in range(2)]
        psW = [stack.enter_context(nc.psum_tensor(f"psW{n}", [P, 512], F32)) for n in range(2)]

        loaded = {n: sem("ld_" + n) for n in
                  ("wq", "wk", "wv", "wo", "heads", "ctx", "mask", "w1", "w2", "b1", "b2")}
        consts = sem("consts")
        identity = sem("identity")
        gaps_zeroed = sem("gaps_zeroed")
        sel_ready = sem("sel_ready")
        bq_ready = sem("bq_ready")
        V_zeroed = sem("V_zeroed")
        pe_wT = sem("pe_wT")
        pe_ctxT = sem("pe_ctxT")
        pe_heads = sem("pe_heads")
        pe_wo_b1 = sem("pe_wo_b1")
        pe_kv = sem("pe_kv")
        pe_M = sem("pe_M")
        pe_c = sem("pe_c")
        pe_V = sem("pe_V")
        pe_sgn = sem("pe_sgn")
        pe_alpha2 = sem("pe_alpha2")
        wT_copied = sem("wT_copied")
        ctxT_copied = sem("ctxT_copied")
        heads_copied = sem("heads_copied")
        wo_copied = sem("wo_copied")
        b1_copied = sem("b1_copied")
        khT_copied = sem("khT_copied")
        vhT_copied = sem("vhT_copied")
        M_copied = sem("M_copied")
        c_copied = sem("c_copied")
        V_copied = sem("V_copied")
        magnitudes1 = sem("magnitudes1")
        magnitudes2 = sem("magnitudes2")
        sgn_steps = sem("sgn_steps")
        sgn1_ready = sem("sgn1_ready")
        sgn2_ready = sem("sgn2_ready")
        sgnT_copied = sem("sgnT_copied")
        top_ready = sem("top_ready")
        top_reduced = sem("top_reduced")
        scale_steps = sem("scale_steps")
        alpha1_ready = sem("alpha1_ready")
        scales_ready = sem("scales_ready")
        diag2_ready = sem("diag2_ready")
        alpha2_ready = sem("alpha2_ready")

        x_loaded = [sem(f"x_loaded{n}") for n in range(2)]
        out_stored = [sem(f"out_stored{n}") for n in range(2)]
        raw_stats = [sem(f"raw_stats{n}") for n in range(2)]
        stats = [sem(f"stats{n}") for n in range(2)]
        norm_steps = [sem(f"norm_steps{n}") for n in range(2)]
        normed = [sem(f"normed{n}") for n in range(2)]
        x_turned = sem("x_turned")
        xT1_copied = sem("xT1_copied")
        scored = sem("scored")
        sc_steps = sem("sc_steps")
        sc_maxed = sem("sc_maxed")
        exped = sem("exped")
        einv_ready = sem("einv_ready")
        e_turned = sem("e_turned")
        eT_copied = sem("eT_copied")
        attended = sem("attended")
        x1_ready = sem("x1_ready")
        x1_turned = sem("x1_turned")
        hi_copied = sem("hi_copied")
        lo_copied = sem("lo_copied")
        y_ready = sem("y_ready")
        gelu_done = sem("gelu_done")
        hi_by_act = sem("hi_by_act")
        hi_by_pool = sem("hi_by_pool")
        h_lo_done = sem("h_lo_done")
        z_added = sem("z_added")
        z_scaled = sem("z_scaled")
        x1b_ready = sem("x1b_ready")
        out_ready = sem("out_ready")

        wait_carrier = sem("wait_carrier")

        block = stack.enter_context(nc.Block())

        def val(i, par, per, n):
            return i * (2 * per) + (per * par + n)

        def dma_val(i, par):
            return i * 16 + 16 * (par // 2 + 1)

        def wait(eng, s, v):
            if not isinstance(v, int) or v > 0:
                eng.wait_ge(s, v)

        def wait_apart(eng, s, v):
            if not isinstance(v, int) or v > 0:
                eng.wait_ge(s, v)
                eng.sem_inc(wait_carrier, 1)

        def is_body(i, par, b):
            return isinstance(i, int) and 2 * i + par == b

        def has(i, par):
            return not isinstance(i, int) or 0 <= 2 * i + par < B

        def pipeline(eng, body, ahead=2):
            pairs = (B - ahead) // 2
            for b in range(-1, 2):
                body(b // 2, b % 2)
            with eng.Fori(1, pairs) as i:
                body(i, 0)
                body(i, 1)
            for b in range(2 * pairs, B + 1):
                body(b // 2, b % 2)

        @block.sync
        def _(sp):
            def rows(w):
                return w.rearrange("(k p) n -> p k n", p=P)

            def load_x(i, par):
                sp.dma_start(x_in[par % 2][:, :, :], x_v[i * 2 + par, :, :, :]) \
                  .then_inc(x_loaded[par % 2], 16)

            sp.dma_start(wk_sb[:, :, :], rows(Wk)).then_inc(loaded["wk"], 16)
            sp.dma_start(ctx_sb[:, :, :], ctx_in.rearrange("b t d -> (b t) d")
                         .rearrange("(n p) d -> p n d", p=P)).then_inc(loaded["ctx"], 16)
            sp.dma_start(wq_sb[:, :, :], rows(Wq)).then_inc(loaded["wq"], 16)
            sp.dma_start(wv_sb[:, :, :], rows(Wv)).then_inc(loaded["wv"], 16)
            load_x(0, 0)
            sp.dma_start(wo_sb[:, :, :], rows(Wo)).then_inc(loaded["wo"], 16)
            sp.dma_start(w1_sb[:, :, :], rows(w1)).then_inc(loaded["w1"], 16)
            sp.dma_start(w2_sb[:, :, :], rows(w2)).then_inc(loaded["w2"], 16)
            load_x(0, 1)

            def body(i, par):
                if has(i, par + 3):
                    wait(sp, x1_ready, val(i, par + 1, 1, 1))
                    load_x(i, par + 3)
                if has(i, par - 1):
                    wait(sp, out_ready, val(i, par - 1, 1, 1))
                    sp.dma_start(out_v[i * 2 + (par - 1), :, :, :], z_sb[(par - 1) % 2][:, :, :]) \
                      .then_inc(out_stored[(par - 1) % 2], 16)

            pipeline(sp, body, ahead=3)
            for s in out_stored:
                sp.wait_ge(s, 16 * (B // 2))

        @block.gpsimd
        def _(pool):
            nc.gpsimd.memset(ident[:, :], 0.0).then_inc(consts, 1)
            nc.gpsimd.memset(ident16[:, :], 0.0).then_inc(consts, 1)
            nc.gpsimd.memset(ones[:, :], 1.0).then_inc(consts, 1)
            nc.gpsimd.memset(mhalf[:, :], -0.5).then_inc(consts, 1)
            nc.gpsimd.memset(masked_sb[:, :, :], MASKED).then_inc(consts, 1)
            pool.wait_ge(consts, 2)
            for m in (ident, ident16):
                nc.gpsimd.affine_select(out=m[:, :], in_=m[:, :], compare_op=ALU.not_equal,
                                        fill=1.0, base=0, pattern=[[-1, P]],
                                        channel_multiplier=1).then_inc(identity, 1)
            pool.wait_ge(consts, 5)
            pool.wait_ge(identity, 2)
            nc.gpsimd.memset(V_sb[0:SK, :, D:], 0.0).then_inc(V_zeroed, 1)
            pool.wait_ge(V_zeroed, 1)
            nc.gpsimd.memset(V_sb[SK:, :, 0:D], 0.0).then_inc(V_zeroed, 1)
            pool.wait_ge(V_zeroed, 2)
            nc.gpsimd.memset(wkvh[:, :, :], 0.0).then_inc(gaps_zeroed, 1)
            nc.gpsimd.memset(sel[:, :], 0.0).then_inc(gaps_zeroed, 1)
            pool.wait_ge(gaps_zeroed, 2)

            def norm(i, par, n, src):
                wait_apart(pool, stats[n], val(i, par, 1, 1))
                nc.gpsimd.tensor_scalar(vare[n][:, :], st[n][:, :, 1], 1.0, EPS, ALU.mult, ALU.add) \
                    .then_inc(norm_steps[n], 1)
                nc.gpsimd.tensor_scalar(nmean[n][:, :], st[n][:, :, 0], -1.0, 1.0, ALU.mult,
                                        ALU.mult).then_inc(norm_steps[n], 1)
                wait(pool, norm_steps[n], val(i, par, 4, 2))
                nc.gpsimd.tensor_tensor(rstd[n][:, :], vare[n][:, :], mhalf[:, :], ALU.pow) \
                    .then_inc(norm_steps[n], 1)
                wait(pool, norm_steps[n], val(i, par, 4, 3))
                nc.gpsimd.tensor_tensor(nmr[n][:, :], nmean[n][:, :], rstd[n][:, :], ALU.mult) \
                    .then_inc(norm_steps[n], 1)
                wait(pool, (x_turned, x1_turned)[n], val(i, par - 1, KD, KD))
                wait_apart(pool, norm_steps[n], val(i, par, 4, 4))
                for j in range(T):
                    last = nc.gpsimd.tensor_scalar(xh[n][:, j, :], src[:, j, :],
                                                   rstd[n][:, j:j + 1], nmr[n][:, j:j + 1],
                                                   ALU.mult, ALU.add)
                last.then_inc(normed[n], 1)

            def top_of_hidden():
                pool.wait_ge(top_ready, 1)
                nc.gpsimd.partition_all_reduce(top_all[:, :], top[:, :], P,
                                               bass.bass_isa.ReduceOp.max).then_inc(top_reduced, 1)

            def hi(i, par, c):
                wait(pool, z_added, val(i, par, C, c - 3))
                wait_apart(pool, gelu_done, val(i, par, C, c + 1))
                nc.gpsimd.tensor_scalar(h_hi[c % 4][:, :], h_sb[c % 4][:, :], h_scale[:, :], 1.0,
                                        ALU.mult, ALU.mult).then_inc(hi_by_pool, 1)

            def body(i, par):
                if is_body(i, par, 0):
                    pool.wait_ge(scales_ready, 1)
                if has(i, par - 1):
                    hi(i, par - 1, 6)
                    hi(i, par - 1, 7)
                if has(i, par):
                    hi(i, par, 0)
                if has(i, par + 2):
                    norm(i, par + 2, 0, x_in[par % 2])
                if has(i, par + 1):
                    norm(i, par + 1, 1, x1)
                if has(i, par):
                    hi(i, par, 5)
                if has(i, par - 1):
                    n = (par - 1) % 2
                    wait(pool, z_scaled, val(i, par - 1, 2, 2))
                    wait(pool, x1b_ready, val(i, par - 1, 1, 1))
                    nc.gpsimd.tensor_tensor(z_sb[n][:, :, :], z_sb[n][:, :, :], x1b[n][:, :, :],
                                            ALU.add).then_inc(out_ready, 1)
                if has(i, par + 1):
                    n = (par + 1) % 2
                    wait(pool, x1_ready, val(i, par + 1, 1, 1))
                    wait(pool, out_ready, val(i, par - 1, 1, 1))
                    for j in range(T):
                        last = nc.gpsimd.tensor_tensor(x1b[n][:, j, :], x1[:, j, :], b2_bc[:, :],
                                                       ALU.add)
                    last.then_inc(x1b_ready, 1)
            norm(0, 0, 0, x_in[0])
            top_of_hidden()
            pool.wait_ge(loaded["b2"], 16)
            pipeline(pool, body)

        @block.scalar
        def _(act):
            act.dma_start(qh_sb[:, :, :], wq_h.rearrange("(k p) h -> p k h", p=P)).then_inc(loaded["heads"], 16)
            act.dma_start(kh_sb[:, :, :], wk_h.rearrange("(k p) h -> p k h", p=P)).then_inc(loaded["heads"], 16)
            act.dma_start(vh_sb[:, :, :], wv_h.rearrange("(k p) h -> p k h", p=P)).then_inc(loaded["heads"], 16)
            for dst, src in ((bq_col[:, :], bq_h), (bk_col[:, :], bk_h), (bv_col[V_AT:, :], bv_h)):
                act.dma_start(dst, src.rearrange("(p a) -> p a", a=1)).then_inc(loaded["heads"], 16)
            act.dma_start(b1_row[:, :], b1.rearrange("(c p) -> c p", p=P)).then_inc(loaded["b1"], 16)
            act.dma_start(mask_sb[:, :, :], mask.rearrange("(p j) t -> p j t", p=P)).then_inc(loaded["mask"], 16)
            act.dma_start(b2_bc[:, :], b2.rearrange("(a n) -> a n", a=1).to_broadcast([P, D])).then_inc(loaded["b2"], 16)

            def copy_V(n):
                act.wait_ge(pe_V, n + 1)
                for h in range(2):
                    part = slice(h * SK, (h + 1) * SK)
                    nc.scalar.activation(V_sb[part, 2 * n:2 * n + 2, h * D:(h + 1) * D],
                                         psY[n % 4][part, :].rearrange("p (b d) -> p b d", b=2),
                                         ACT.Copy).then_inc(V_copied, 1)

            def exp(i, par):
                wait(act, sc_maxed, val(i, par, 1, 1))
                wait(act, e_turned, val(i, par - 1, 1, 1))
                wait(act, einv_ready, val(i, par - 1, 1, 1))
                for j in range(T):
                    last = nc.scalar.activation(e_sb[:, j, :], sc[:, j, :], ACT.Exp,
                                                bias=nmax[:, j:j + 1], scale=1.0,
                                                accum_out=esum[:, j:j + 1])
                last.then_inc(exped, 1)

            def gelu(i, par, c):
                wait(act, y_ready, val(i, par, C, c + 1))
                wait(act, h_lo_done, val(i, par, C, c - 3))
                nc.scalar.activation(h_sb[c % 4][:, :], psY[c % 4][:, :], ACT.Gelu,
                                     bias=b1_col[:, c:c + 1], scale=alpha1x[:, c:c + 1]) \
                    .then_inc(gelu_done, 1)

            def hi(i, par, c):
                wait(act, gelu_done, val(i, par, C, c + 1))
                wait(act, z_added, val(i, par, C, c - 3))
                nc.scalar.activation(h_hi[c % 4][:, :], h_sb[c % 4][:, :], ACT.Copy,
                                     scale=h_scale[:, :]).then_inc(hi_by_act, 1)

            def copy_xT(i, par):
                wait(act, scored, val(i, par - 1, 1, 1))
                for k in range(KD):
                    wait(act, x_turned, val(i, par, KD, k + 1))
                    nc.scalar.activation(xT1[:, k, :], psW[k][:, :], ACT.Copy).then_inc(xT1_copied, 1)

            for n, w in enumerate((wkT, wqT, wvT)):
                act.wait_ge(pe_wT, n + 1)
                nc.scalar.activation(w[:, :, :].rearrange("p k n -> p (k n)"), psY[n][:, :],
                                     ACT.Copy).then_inc(wT_copied, 1)
            copy_xT(0, 0)
            for m, (k, n) in enumerate((k, n) for n in range(NH) for k in range(KD)):
                act.wait_ge(pe_M, m + 1)
                nc.scalar.activation(M_sb[:, k, n * HALF:(n + 1) * HALF],
                                     (psY[2], psY[3], psZ[0], psZ[1])[m][:, :],
                                     ACT.Copy).then_inc(M_copied, 1)
            act.wait_ge(loaded["w1"], 16)
            for c in range(C):
                last = nc.scalar.activation(magnitudes[:, c * D:(c + 1) * D], w1_sb[:, c, :], ACT.Abs,
                                            accum_out=abs1[:, c:c + 1])
            last.then_inc(magnitudes1, 1)
            act.wait_ge(V_zeroed, 2)
            copy_V(0)
            copy_V(1)
            exp(0, 0)
            act.wait_ge(loaded["w2"], 16)
            act.wait_ge(magnitudes1, 1)
            for k in range(KD):
                last = nc.scalar.activation(magnitudes[:, k * H:(k + 1) * H], w2_sb[:, k, :], ACT.Abs,
                                            accum_out=abs2[:, k:k + 1])
            last.then_inc(magnitudes2, 1)
            copy_V(2)
            copy_V(3)

            def body(i, par):
                late, early, ffn, prev = (has(i, par + d) for d in (1, 2, 0, -1))
                if prev:
                    gelu(i, par - 1, 6)
                    gelu(i, par - 1, 7)
                if late:
                    wait(act, e_turned, val(i, par + 1, 1, 1))
                    wait(act, attended, val(i, par, 2, 2))
                    nc.scalar.activation(eT[:, :, :].rearrange("p n t -> p (n t)"),
                                         psW[0][:, 0:T // 2 * P], ACT.Copy).then_inc(eT_copied, 1)
                if ffn:
                    if is_body(i, par, 0):
                        act.wait_ge(alpha1_ready, 1)
                        act.wait_ge(b1_copied, 1)
                        act.wait_ge(scales_ready, 1)
                    gelu(i, par, 0)
                    gelu(i, par, 1)
                    hi(i, par, 1)
                    gelu(i, par, 2)
                    hi(i, par, 2)
                    gelu(i, par, 3)
                    hi(i, par, 3)
                    gelu(i, par, 4)
                if early:
                    copy_xT(i, par + 2)
                if is_body(i, par, -1):
                    for n in range(4, B // 2):
                        copy_V(n)
                if ffn:
                    hi(i, par, 4)
                    gelu(i, par, 5)
                if late:
                    n = (par + 1) % 2
                    wait(act, y_ready, val(i, par - 1, C, C))
                    for m, k in enumerate(reversed(range(KD))):
                        wait(act, x1_turned, val(i, par + 1, KD, m + 1))
                        nc.scalar.activation(x_hi[n][:, k, :], psW[k][:, :], ACT.Copy,
                                             scale=X_SCALE).then_inc(hi_copied, 1)
                if early:
                    exp(i, par + 2)

            pipeline(act, body)

        @block.vector
        def _(dve):
            def raw_bn(n, src):
                for j in range(T):
                    last = nc.vector.bn_stats(st_raw[n][:, j, :], src[:, j, :])
                return last

            def bn(i, par, n):
                wait(dve, normed[n], val(i, par - 1, 1, 1))
                wait_apart(dve, raw_stats[n], val(i, par, 1, 1))
                for j in range(T):
                    last = nc.vector.bn_aggr(st[n][:, j, :], st_raw[n][:, j, :])
                last.then_inc(stats[n], 1)

            def lo(i, par, c):
                owner, chunks = (hi_by_act, ACT_HI) if c in ACT_HI else (hi_by_pool, POOL_HI)
                wait(dve, owner, val(i, par, len(chunks), chunks.index(c) + 1))
                nc.vector.scalar_tensor_tensor(out=h_lo[c % 4][:, :], in0=h_sb[c % 4][:, :],
                                               scalar=h_scale[:, :], in1=h_hi[c % 4][:, :],
                                               op0=ALU.mult, op1=ALU.subtract).then_inc(h_lo_done, 1)

            def scores(i, par):
                wait(dve, scored, val(i, par, 1, 1))
                wait(dve, exped, val(i, par - 1, 1, 1))
                b0 = i * (2 * SK) + par * SK
                nc.vector.tensor_tensor(
                    sc[:, :, :], psW[0][:, 0:T * SK].rearrange("p (j t) -> p j t", j=T),
                    c_sb[:, bass.ds(b0, SK)].unsqueeze(1).to_broadcast([P, T, SK]), ALU.add) \
                    .then_inc(sc_steps, 1)
                wait_apart(dve, sc_steps, val(i, par, 2, 1))
                nc.vector.copy_predicated(sc[:, :, :], mask_sb[:, :, :], masked_sb[:, :, :]) \
                    .then_inc(sc_steps, 1)
                wait(dve, sc_steps, val(i, par, 2, 2))
                nc.vector.tensor_reduce(nmax[:, :], sc[:, :, :], AX.X, ALU.max, negate=True) \
                    .then_inc(sc_maxed, 1)

            def first_norm(i, par):
                n = par % 2
                wait(dve, x_loaded[n], dma_val(i, par))
                raw_bn(0, x_in[n]).then_inc(raw_stats[0], 1)
                bn(i, par, 0)

            def minus_where_negative(neg, w_flat):
                nc.vector.tensor_scalar(neg[:, :], w_flat, 0.0, None, ALU.is_lt).then_inc(sgn_steps, 1)

            def signs(sgn, neg, w_flat, step, ready):
                dve.wait_ge(sgn_steps, step)
                nc.vector.scalar_tensor_tensor(out=sgn[:, :], in0=w_flat, scalar=0.0, in1=neg[:, :],
                                               op0=ALU.is_gt, op1=ALU.subtract).then_inc(ready, 1)

            w1_flat = w1_sb[:, :, :].rearrange("p c d -> p (c d)")
            w2_flat = w2_sb[:, :, :].rearrange("p k n -> p (k n)")

            dve.wait_ge(identity, 1)
            dve.wait_ge(gaps_zeroed, 2)
            nc.vector.tensor_reduce(sel[:, V_AT:], ident[:, :].rearrange("p (g h) -> p h g", h=HD),
                                    AX.X, ALU.add).then_inc(sel_ready, 1)
            dve.wait_ge(loaded["heads"], 96)
            dve.wait_ge(consts, 5)
            nc.vector.tensor_scalar(bq_rep[:, :], ones[0:HD, :], bq_col[:, :], None,
                                    ALU.mult).then_inc(bq_ready, 1)
            for k in range(KD):
                for n in range(NH):
                    m = k * NH + n
                    dve.wait_ge(pe_ctxT, m + 1)
                    nc.vector.tensor_copy(ctxT[:, k, n * HALF:(n + 1) * HALF],
                                          (psZ[0], psZ[1], psW[0], psW[1])[m][:, :]) \
                        .then_inc(ctxT_copied, 1)
            first_norm(0, 0)
            dve.wait_ge(pe_heads, 1)
            for at, m in ((0, 0), (V_AT, 1)):
                nc.vector.tensor_copy(wkvh[:, :, at:at + HD],
                                      psY[3][:, D + m * KD * HD:D + (m + 1) * KD * HD]
                                      .rearrange("p (k h) -> p k h", k=KD)).then_inc(heads_copied, 1)
            nc.vector.tensor_copy(wqhT[:, :], psY[3][0:HD, 0:D]).then_inc(heads_copied, 1)
            dve.wait_ge(pe_wo_b1, 1)
            nc.vector.tensor_copy(wo_sum[V_AT:, :], psW[0][V_AT:V_AT + HD, 0:D]).then_inc(wo_copied, 1)
            nc.vector.tensor_copy(b1_col[:, :], psW[0][:, D:D + C]).then_inc(b1_copied, 1)
            dve.wait_ge(loaded["w1"], 16)
            minus_where_negative(neg1, w1_flat)
            for n in range(NH):
                dve.wait_ge(pe_kv, n + 1)
                nc.vector.tensor_scalar(khT[:, n * HALF:(n + 1) * HALF], psY[n][0:HD, :],
                                        bk_col[:, :], SCORE_SCALE, ALU.add, ALU.mult) \
                    .then_inc(khT_copied, 1)
                for h in range(2):
                    nc.vector.tensor_scalar(vhT[V_AT:, n * (B // 2):(n + 1) * (B // 2), h, :],
                                            psY[n][V_AT:V_AT + HD, :].rearrange("p (b t) -> p b t", t=SK),
                                            bv_col[V_AT:, :], None, ALU.add).then_inc(vhT_copied, 1)
            signs(sgn1, neg1, w1_flat, 1, sgn1_ready)
            for n in range(NH):
                dve.wait_ge(pe_c, n + 1)
                nc.vector.tensor_copy(c_sb[:, n * HALF:(n + 1) * HALF], psY[n][:, :]).then_inc(c_copied, 1)
            dve.wait_ge(magnitudes1, 1)
            nc.vector.tensor_scalar(alpha1x[:, :], abs1[:, :], 1.0 / (D * X_SCALE), None,
                                    ALU.mult).then_inc(alpha1_ready, 1)
            dve.wait_ge(b1_copied, 1)
            nc.vector.scalar_tensor_tensor(out=b1_abs[:, :], in0=b1_col[:, :], scalar=-1.0,
                                           in1=b1_col[:, :], op0=ALU.mult, op1=ALU.max) \
                .then_inc(scale_steps, 1)
            dve.wait_ge(scale_steps, 1)
            nc.vector.scalar_tensor_tensor(out=bound[:, :], in0=abs1[:, :], scalar=1.001,
                                           in1=b1_abs[:, :], op0=ALU.mult, op1=ALU.add) \
                .then_inc(scale_steps, 1)
            dve.wait_ge(scale_steps, 2)
            nc.vector.tensor_reduce(top[:, :], bound[:, :], AX.X, ALU.max).then_inc(top_ready, 1)
            dve.wait_ge(c_copied, 2)
            dve.wait_ge(loaded["mask"], 16)
            scores(0, 0)
            dve.wait_ge(loaded["w2"], 16)
            minus_where_negative(neg2, w2_flat)
            dve.wait_ge(top_reduced, 1)
            nc.vector.tensor_scalar(top[:, :], top_all[:, :], LEAST_BOUND, None, ALU.max) \
                .then_inc(scale_steps, 1)
            dve.wait_ge(scale_steps, 3)
            nc.vector.tensor_scalar(pow2[:, :].bitcast(U32), top[:, :].bitcast(U32), 0x7F800000,
                                    None, ALU.bitwise_and).then_inc(scale_steps, 1)
            signs(sgn2, neg2, w2_flat, 2, sgn2_ready)
            dve.wait_ge(scale_steps, 4)
            nc.vector.reciprocal(inv_pow2[:, :], pow2[:, :]).then_inc(scale_steps, 1)
            nc.vector.tensor_scalar(h_unscale[:, :], pow2[:, :], 1.0 / H_TOP, None,
                                    ALU.mult).then_inc(scale_steps, 1)
            dve.wait_ge(scale_steps, 6)
            nc.vector.tensor_scalar(h_scale[:, :], inv_pow2[:, :], H_TOP, None,
                                    ALU.mult).then_inc(scales_ready, 1)
            dve.wait_ge(magnitudes2, 1)
            for k in range(KD):
                nc.vector.tensor_scalar(diag2[:, k, :], ident[:, :], abs2[:, k:k + 1], 1.0 / H,
                                        ALU.mult, ALU.mult).then_inc(diag2_ready, 1)

            def copy_signs():
                for n in range(4):
                    dve.wait_ge(pe_sgn, n + 1)
                    dst = (sgn1T[:, 0, :], sgn1T[:, 1, :],
                           sgn2T[:, 0:4, :].rearrange("p c d -> p (c d)"),
                           sgn2T[:, 4:8, :].rearrange("p c d -> p (c d)"))[n]
                    nc.vector.tensor_copy(dst, (psZ[0], psZ[1], psZ[0], psZ[1])[n][:, :].bitcast(F16)) \
                        .then_inc(sgnT_copied, 1)
                dve.wait_ge(pe_alpha2, 1)
                nc.vector.tensor_scalar(alpha2_bc[:, :], psZ[0][:, 0:D], h_unscale[:, :], None,
                                        ALU.mult).then_inc(alpha2_ready, 1)

            def body(i, par):
                late, early, ffn, prev = (has(i, par + d) for d in (1, 2, 0, -1))
                if early:
                    first_norm(i, par + 2)
                if late:
                    wait(dve, exped, val(i, par + 1, 1, 1))
                    nc.vector.reciprocal(einv[:, :], esum[:, :]).then_inc(einv_ready, 1)
                if prev:
                    lo(i, par - 1, 6)
                    lo(i, par - 1, 7)
                if ffn:
                    if is_body(i, par, 0):
                        dve.wait_ge(scales_ready, 1)
                        dve.wait_ge(alpha2_ready, 1)
                    lo(i, par, 0)
                    lo(i, par, 1)
                if prev:
                    m = (par - 1) % 2
                    wait(dve, z_added, val(i, par - 1, C, C))
                    wait(dve, out_stored[m], dma_val(i, par - 3))
                    for n in range(2):
                        nc.vector.tensor_tensor(
                            z_sb[m][:, 2 * n:2 * n + 2, :],
                            psZ[n][:, :].rearrange("p (j d) -> p j d", j=2),
                            alpha2_bc[:, :].unsqueeze(1).to_broadcast([P, 2, D]), ALU.mult) \
                            .then_inc(z_scaled, 1)
                if late:
                    m = (par + 1) % 2
                    wait(dve, einv_ready, val(i, par + 1, 1, 1))
                    wait(dve, x1b_ready, val(i, par, 1, 1))
                    for j in range(T):
                        if j % 2 == 0:
                            wait(dve, attended, val(i, par + 1, 2, j // 2 + 1))
                        last = nc.vector.scalar_tensor_tensor(
                            out=x1[:, j, :], in0=psW[j // 2][:, (j % 2) * D:(j % 2 + 1) * D],
                            scalar=einv[:, j:j + 1], in1=x_in[m][:, j, :], op0=ALU.mult, op1=ALU.add)
                    last.then_inc(x1_ready, 1)
                    wait(dve, x1_ready, val(i, par + 1, 1, 1))
                    raw_bn(1, x1).then_inc(raw_stats[1], 1)
                    bn(i, par + 1, 1)
                if is_body(i, par, -1):
                    copy_signs()
                if ffn:
                    lo(i, par, 2)
                    lo(i, par, 3)
                    lo(i, par, 4)
                if early:
                    scores(i, par + 2)
                if ffn:
                    lo(i, par, 5)
                if late:
                    m = (par + 1) % 2
                    for n, k in enumerate(reversed(range(KD))):
                        wait(dve, hi_copied, val(i, par + 1, KD, n + 1))
                        nc.vector.scalar_tensor_tensor(out=x_lo[m][:, k, :], in0=psW[k][:, :],
                                                       scalar=X_SCALE, in1=x_hi[m][:, k, :],
                                                       op0=ALU.mult, op1=ALU.subtract) \
                            .then_inc(lo_copied, 1)

            pipeline(dve, body)

        @block.tensor
        def _(pe):
            def turn_square(n, w, name):
                pe.wait_ge(loaded[name], 16)
                for k in range(KD):
                    for m in range(KD):
                        last = nc.tensor.transpose(psY[n][:, k * D + m * P:k * D + (m + 1) * P],
                                                   w[:, m, k * P:(k + 1) * P], ident[:, :])
                last.then_inc(pe_wT, 1)

            def turn_context():
                pe.wait_ge(loaded["ctx"], 16)
                for k in range(KD):
                    for h in range(NH):
                        ps = (psZ[0], psZ[1], psW[0], psW[1])[k * NH + h]
                        for t in range(HALF // P):
                            last = nc.tensor.transpose(ps[:, t * P:(t + 1) * P],
                                                       ctx_sb[:, h * (HALF // P) + t, k * P:(k + 1) * P],
                                                       ident[:, :])
                        last.then_inc(pe_ctxT, 1)

            def head_weights():
                pe.wait_ge(loaded["heads"], 96)
                pe.wait_ge(wT_copied, 3)
                for n, (wT, hd) in enumerate(((wkT, kh_sb), (wvT, vh_sb))):
                    for m in range(KD):
                        at = D + (n * KD + m) * HD
                        for k in range(KD):
                            nc.tensor.matmul(psY[3][:, at:at + HD], wT[:, k, m * P:(m + 1) * P],
                                             hd[:, k, :], start=(k == 0), stop=(k == KD - 1))
                for k in range(KD):
                    last = nc.tensor.matmul(psY[3][0:HD, 0:D], qh_sb[:, k, :], wqT[:, k, :],
                                            start=(k == 0), stop=(k == KD - 1))
                last.then_inc(pe_heads, 1)

            def wo_blocks_and_b1():
                pe.wait_ge(sel_ready, 1)
                pe.wait_ge(loaded["wo"], 16)
                pe.wait_ge(loaded["b1"], 16)
                pe.wait_ge(ctxT_copied, 3)
                for k in range(KD):
                    nc.tensor.matmul(psW[0][0:V_AT + HD, 0:D], sel[:, :], wo_sb[:, k, :],
                                     start=(k == 0), stop=(k == KD - 1))
                nc.tensor.transpose(psW[0][:, D:D + C], b1_row[:, :], ident[0:C, 0:C]).then_inc(pe_wo_b1, 1)

            def keys_and_values():
                pe.wait_ge(heads_copied, 3)
                pe.wait_ge(ctxT_copied, 4)
                for n in range(NH):
                    for k in range(KD):
                        last = nc.tensor.matmul(psY[n][0:V_AT + HD, :], wkvh[:, k, :],
                                                ctxT[:, k, n * HALF:(n + 1) * HALF],
                                                start=(k == 0), stop=(k == KD - 1))
                    last.then_inc(pe_kv, 1)

            def score_weights():
                for m, (k, n) in enumerate((k, n) for n in range(NH) for k in range(KD)):
                    pe.wait_ge(khT_copied, n + 1)
                    nc.tensor.matmul((psY[2], psY[3], psZ[0], psZ[1])[m][:, :],
                                     wqhT[:, k * P:(k + 1) * P], khT[:, n * HALF:(n + 1) * HALF],
                                     start=True, stop=True).then_inc(pe_M, 1)
                pe.wait_ge(bq_ready, 1)
                for n in range(NH):
                    pe.wait_ge(vhT_copied, 2 * n + 2)
                    nc.tensor.matmul(psY[n][:, :], bq_rep[:, :], khT[:, n * HALF:(n + 1) * HALF],
                                     start=True, stop=True).then_inc(pe_c, 1)

            def values(n):
                if n == 0:
                    pe.wait_ge(wo_copied, 1)
                    pe.wait_ge(vhT_copied, 4)
                if n < 2:
                    pe.wait_ge(c_copied, n + 1)
                elif n < 4:
                    pe.wait_ge(M_copied, n - 1)
                else:
                    pe.wait_ge(V_copied, 2 * (n - 3))
                for m in range(2):
                    last = nc.tensor.matmul(psY[n % 4][:, m * D:(m + 1) * D],
                                            vhT[V_AT:, 2 * n + m, :, :].rearrange("p h t -> p (h t)"),
                                            wo_sum[V_AT:, :], start=True, stop=True)
                last.then_inc(pe_V, 1)

            def turn_signs():
                pe.wait_ge(sgn1_ready, 1)
                pe.wait_ge(M_copied, 4)
                for k in range(KD):
                    ps = psZ[k][:, :].bitcast(F16)
                    for c in range(C):
                        last = nc.tensor.transpose(ps[:, c * P:(c + 1) * P],
                                                   sgn1[:, c * D + k * P:c * D + (k + 1) * P], ident16[:, :])
                    last.then_inc(pe_sgn, 1)
                pe.wait_ge(sgn2_ready, 1)
                for n in range(2):
                    pe.wait_ge(sgnT_copied, n + 1)
                    ps = psZ[n][:, :].bitcast(F16)
                    for c in range(4):
                        for k in range(KD):
                            a = k * H + (4 * n + c) * P
                            last = nc.tensor.transpose(ps[:, c * D + k * P:c * D + (k + 1) * P],
                                                       sgn2[:, a:a + P], ident16[:, :])
                    last.then_inc(pe_sgn, 1)
                pe.wait_ge(diag2_ready, 2)
                pe.wait_ge(sgnT_copied, 3)
                for k in range(KD):
                    last = nc.tensor.matmul(psZ[0][:, k * P:(k + 1) * P], ones[:, :], diag2[:, k, :],
                                            start=True, stop=True)
                last.then_inc(pe_alpha2, 1)

            def turn_x(i, par, n):
                wait(pe, normed[n], val(i, par, 1, 1))
                if n == 0:
                    wait(pe, x1_ready, val(i, par - 1, 1, 1))
                else:
                    wait(pe, xT1_copied, val(i, par + 1, KD, KD) if has(i, par + 1) else 0)
                    wait(pe, x1_ready, val(i, par, 1, 1))
                for k in (range(KD) if n == 0 else reversed(range(KD))):
                    if n == 1 and k == 0 and has(i, par + 1):
                        wait(pe, sc_steps, val(i, par + 1, 2, 1))
                    for j in range(T):
                        last = nc.tensor.transpose(psW[k][:, j * P:(j + 1) * P],
                                                   xh[n][:, j, k * P:(k + 1) * P], ident[:, :])
                    last.then_inc((x_turned, x1_turned)[n], 1)

            def score(i, par):
                wait(pe, xT1_copied, val(i, par, KD, KD))
                b0 = i * (2 * SK) + par * SK
                for j in range(T):
                    for k in range(KD):
                        last = nc.tensor.matmul(psW[0][:, j * SK:(j + 1) * SK], xT1[:, k, j * P:(j + 1) * P],
                                                M_sb[:, k, bass.ds(b0, SK)], start=(k == 0), stop=(k == KD - 1))
                last.then_inc(scored, 1)

            def turn_e(i, par):
                wait(pe, exped, val(i, par, 1, 1))
                wait(pe, lo_copied, val(i, par - 1, KD, KD))
                for n in range(T // 2):
                    last = nc.tensor.transpose(psW[0][:, n * P:(n + 1) * P],
                                               e_sb[:, 2 * n:2 * n + 2, :].rearrange("p j t -> p (j t)"),
                                               ident[:, :])
                last.then_inc(e_turned, 1)

            def attend(i, par):
                wait(pe, eT_copied, val(i, par, 1, 1))
                wait(pe, lo_copied, val(i, par - 1, KD, KD))
                wait(pe, xT1_copied, val(i, par, KD, KD))
                for n in range(T // 2):
                    nc.tensor.matmul(psW[n][:, :], eT[:, n, :], V_sb[:, i * 2 + par, :],
                                     start=True, stop=True).then_inc(attended, 1)

            def first_product(i, par, c):
                if c == 0:
                    wait(pe, lo_copied, val(i, par, KD, KD))
                wait(pe, gelu_done, val(i, par, C, c - 3))
                slot = par % 2
                n = 0
                for k in range(KD):
                    for part in (x_hi, x_lo):
                        last = nc.tensor.matmul(psY[c % 4][:, :], sgn1T[:, k, c * P:(c + 1) * P],
                                                part[slot][:, k, :], start=(n == 0), stop=(n == 2 * KD - 1))
                        n += 1
                last.then_inc(y_ready, 1)

            def second_product(i, par, c):
                wait(pe, h_lo_done, val(i, par, C, c + 1))
                if c == 0:
                    wait(pe, z_scaled, val(i, par - 1, 2, 2))
                for j in range(T):
                    for n, part in enumerate((h_hi, h_lo)):
                        last = nc.tensor.matmul(psZ[j // 2][:, (j % 2) * D:(j % 2 + 1) * D],
                                                part[c % 4][:, j * P:(j + 1) * P], sgn2T[:, c, :],
                                                start=(c == 0 and n == 0 and j % 2 == 0),
                                                stop=(c == C - 1 and n == 1 and j % 2 == 1))
                last.then_inc(z_added, 1)

            def body(i, par):
                late, early, ffn, prev = (has(i, par + d) for d in (1, 2, 0, -1))
                if is_body(i, par, 0):
                    pe.wait_ge(V_copied, B)
                    pe.wait_ge(sgnT_copied, 4)
                    pe.wait_ge(alpha2_ready, 1)
                if ffn:
                    first_product(i, par, 0)
                if late:
                    turn_e(i, par + 1)
                for c in range(3):
                    if prev:
                        second_product(i, par - 1, C - 3 + c)
                    if ffn and c < 2:
                        first_product(i, par, c + 1)
                if late:
                    attend(i, par + 1)
                if ffn:
                    first_product(i, par, 3)
                    second_product(i, par, 0)
                    first_product(i, par, 4)
                if early:
                    turn_x(i, par + 2, 0)
                if ffn:
                    second_product(i, par, 1)
                    first_product(i, par, 5)
                if early:
                    score(i, par + 2)
                if is_body(i, par, -1):
                    for n in range(4, B // 2):
                        values(n)
                    turn_signs()
                if late:
                    turn_x(i, par + 1, 1)
                if ffn:
                    second_product(i, par, 2)
                    first_product(i, par, 6)
                    second_product(i, par, 3)
                    first_product(i, par, 7)
                    second_product(i, par, 4)

            pe.wait_ge(identity, 2)
            pe.wait_ge(consts, 5)
            turn_square(0, wk_sb, "wk")
            turn_context()
            turn_square(1, wq_sb, "wq")
            turn_square(2, wv_sb, "wv")
            head_weights()
            wo_blocks_and_b1()
            keys_and_values()
            pe.wait_ge(wo_copied, 1)
            pe.wait_ge(b1_copied, 1)
            turn_x(0, 0, 0)
            score_weights()
            pe.wait_ge(M_copied, 4)
            score(0, 0)
            for n in range(4):
                values(n)
            pipeline(pe, body)


_INS = ['x', 'ctx_1024', 'mask_SxS2_bk1', 'L0_xattn_Wq', 'L0_xattn_Wk', 'L0_xattn_Wv', 'L0_xattn_wq_h',
        'L0_xattn_bq_h', 'L0_xattn_wk_h', 'L0_xattn_bk_h', 'L0_xattn_wv_h', 'L0_xattn_bv_h',
        'L0_xattn_Wo', 'L0_ffn_w1', 'L0_ffn_b1', 'L0_ffn_w2', 'L0_ffn_b2']


def kernel(**inputs):
    import numpy as _np
    import concourse.bacc as _bacc
    from concourse import mybir as _mybir
    from concourse.bass_utils import run_bass_kernel_spmd as _run

    nc = _bacc.Bacc("TRN2", target_bir_lowering=False, num_devices=1)
    arrays, args = {}, []
    for name in _INS:
        a = _np.ascontiguousarray(inputs[name])
        arrays[f"in_{name}"] = a
        args.append(nc.dram_tensor(f"in_{name}", a.shape, _mybir.dt.from_np(a.dtype), kind="ExternalInput").ap())
    out = nc.dram_tensor("out_x", arrays["in_x"].shape, _mybir.dt.float32, kind="ExternalOutput").ap()
    xattn_ffn_kernel(nc, *args, out)
    r = _run(nc, [arrays], core_ids=[0])
    return r.results[0]["out_x"]
```

```python
from contextlib import ExitStack

import concourse.bass as bass
from concourse import mybir

ALU = mybir.AluOpType
ACT = mybir.ActivationFunctionType
AX = mybir.AxisListType
F32 = mybir.dt.float32
F16 = mybir.dt.float16
BF16 = mybir.dt.bfloat16
U32 = mybir.dt.uint32
U8 = mybir.dt.uint8

P = 128
EPS = 1e-5
MASKED = -1000000000.0
X_SCALE = 2048.0
H_TOP = 2.0 ** 14
E_SCALE = 2.0 ** 15
MV_TOP = 2.0 ** 10
LEAST_BOUND = 1e-20


def xattn_ffn_kernel(nc, x, ctx_in, mask, Wq, Wk, Wv, wq_h, bq_h, wk_h, bk_h, wv_h, bv_h, Wo,
                     w1, b1, w2, b2, out):
    B, S, D = x.shape
    SK = ctx_in.shape[1]
    HD = wq_h.shape[1]
    H = w1.shape[0]
    T = S // P
    KD = D // P
    C = H // P
    KT = B * SK // P
    HALF = 512
    NH = B * SK // HALF
    SCORE_SCALE = float(HD) ** -0.5
    V_AT = 32
    POOL_HI = (1, 5, 6, 7)
    ACT_HI = (0, 2, 3, 4)
    TAIL = 2
    assert S == 512 and D == 256 and SK == 64 and HD == 16 and C == 8 and B % 2 == 0 and NH == 2

    x_v = x.rearrange("b (p j) d -> b p j d", p=P)
    out_v = out.rearrange("b (p j) d -> b p j d", p=P)

    with ExitStack() as stack:
        def sb(name, shape, dt=F32):
            return stack.enter_context(nc.sbuf_tensor(name, shape, dt))

        def sem(name):
            return stack.enter_context(nc.semaphore(name))

        ident = sb("ident", [P, P])
        ident16 = sb("ident16", [P, P], F16)
        ones = sb("ones", [P, P])
        sel = sb("sel", [P, V_AT + HD])
        wq_sb = sb("wq_sb", [P, KD, D])
        wk_sb = sb("wk_sb", [P, KD, D])
        wv_sb = sb("wv_sb", [P, KD, D])
        wo_sb = sb("wo_sb", [P, KD, D])
        wqT = sb("wqT", [P, KD, D])
        wkT = sb("wkT", [P, KD, D])
        wvT = sb("wvT", [P, KD, D])
        qh_sb = sb("qh_sb", [P, KD, HD])
        kh_sb = sb("kh_sb", [P, KD, HD])
        vh_sb = sb("vh_sb", [P, KD, HD])
        bq_col = sb("bq_col", [HD, 1])
        bk_col = sb("bk_col", [HD, 1])
        bv_col = sb("bv_col", [V_AT + HD, 1])
        bias_abs = sb("bias_abs", [V_AT + HD, 1])
        kv_max = sb("kv_max", [V_AT + HD, NH + 1])
        bq_rep = sb("bq_rep", [HD, P])
        ctx_sb = sb("ctx_sb", [P, KT, D])
        ctxT = sb("ctxT", [P, KD, B * SK])
        wqhT = sb("wqhT", [HD, D])
        wkvh = sb("wkvh", [P, KD, V_AT + HD])
        wo_sum = sb("wo_sum", [V_AT + HD, D])
        khT = sb("khT", [HD, B * SK])
        vhT = sb("vhT", [V_AT + HD, B, 2, SK])
        M_hl = sb("M_hl", [P, KD, B, 2, SK], F16)
        c_sb = sb("c_sb", [P, B * SK])
        V_hl = sb("V_hl", [P, B, 2, D], F16)
        mask_sb = sb("mask_sb", [P, T, SK], U8)
        masked_sb = sb("masked_sb", [P, T, SK])
        w1_sb = sb("w1_sb", [P, C, D])
        w2_sb = sb("w2_sb", [P, KD, H])
        neg1 = sb("neg1", [P, C * D], F16)
        neg2 = sb("neg2", [P, KD * H], F16)
        sgn1 = sb("sgn1", [P, C * D], F16)
        sgn2 = sb("sgn2", [P, KD * H], F16)
        sgn1T = sb("sgn1T", [P, KD, H], F16)
        sgn2T = sb("sgn2T", [P, C, D], F16)
        b1_col = sb("b1_col", [P, C])
        b1_row = sb("b1_row", [C, P])
        b2_bc = sb("b2_bc", [P, D])
        abs1 = sb("abs1", [P, C])
        alpha1x = sb("alpha1x", [P, C])
        bound = sb("bound", [P, C])
        b1_abs = sb("b1_abs", [P, C])
        top = sb("top", [P, 1])
        top_all = sb("top_all", [P, 1])
        pow2 = sb("pow2", [P, 1])
        inv_pow2 = sb("inv_pow2", [P, 1])
        h_scale = sb("h_scale", [P, 1])
        h_unscale = sb("h_unscale", [P, 1])
        abs2 = sb("abs2", [P, KD])
        diag2 = sb("diag2", [P, KD, P])
        alpha2_bc = sb("alpha2_bc", [P, D])
        mags = sb("mags", [P, 4])
        mags_all = sb("mags_all", [P, 4])
        mv_bound = sb("mv_bound", [P, 2])
        mv_pow2 = sb("mv_pow2", [P, 2])
        mv_inv = sb("mv_inv", [P, 2])
        mv_scale = sb("mv_scale", [P, 2])
        score_unscale = sb("score_unscale", [P, 1])
        mhalf = sb("mhalf", [P, T])
        magnitudes = sb("magnitudes", [P, C * D], BF16)

        x_in = [sb(f"x_in{n}", [P, T, D]) for n in range(2)]
        st_raw = [sb(f"st_raw{n}", [P, T, 6]) for n in range(2)]
        st = [sb(f"st{n}", [P, T, 2]) for n in range(2)]
        nmean = [sb(f"nmean{n}", [P, T]) for n in range(2)]
        vare = [sb(f"vare{n}", [P, T]) for n in range(2)]
        rstd = [sb(f"rstd{n}", [P, T]) for n in range(2)]
        nmr = [sb(f"nmr{n}", [P, T]) for n in range(2)]
        xh = [sb(f"xh{n}", [P, T, D]) for n in range(2)]
        xT_hi = sb("xT_hi", [P, KD, S], F16)
        xT_lo = sb("xT_lo", [P, KD, S], F16)
        sc = sb("sc", [P, T, SK])
        nmax = sb("nmax", [P, T])
        e_sb = sb("e_sb", [P, T, SK])
        e_hl = sb("e_hl", [P, T, 2, SK], F16)
        esum = sb("esum", [P, T])
        esum_scaled = sb("esum_scaled", [P, T])
        einv = sb("einv", [P, T])
        eT = sb("eT", [P, T, P], F16)
        x1 = sb("x1", [P, T, D])
        x1b = [sb(f"x1b{n}", [P, T, D]) for n in range(2)]
        x_hi = [sb(f"x_hi{n}", [P, KD, S], F16) for n in range(2)]
        x_lo = [sb(f"x_lo{n}", [P, KD, S], F16) for n in range(2)]
        h_sb = [sb(f"h_sb{n}", [P, S]) for n in range(4)]
        h_hi = [sb(f"h_hi{n}", [P, S], F16) for n in range(4)]
        h_lo = [sb(f"h_lo{n}", [P, S], F16) for n in range(4)]
        z_sb = [sb(f"z_sb{n}", [P, T, D]) for n in range(2)]

        psY = [stack.enter_context(nc.psum_tensor(f"psY{n}", [P, 512], F32)) for n in range(4)]
        psZ = [stack.enter_context(nc.psum_tensor(f"psZ{n}", [P, 512], F32)) for n in range(2)]
        psW = [stack.enter_context(nc.psum_tensor(f"psW{n}", [P, 512], F32)) for n in range(2)]

        loaded = {n: sem("ld_" + n) for n in
                  ("wq", "wk", "wv", "wo", "kq_heads", "v_head", "biases", "ctx", "mask", "w1", "w2", "b1", "b2")}
        consts = sem("consts")
        identity = sem("identity")
        gaps_zeroed = sem("gaps_zeroed")
        sel_ready = sem("sel_ready")
        bq_ready = sem("bq_ready")
        bias_abs_ready = sem("bias_abs_ready")
        kv_maxed = sem("kv_maxed")
        mags_ready = sem("mags_ready")
        mags_reduced = sem("mags_reduced")
        mv_steps = sem("mv_steps")
        mv_scales_ready = sem("mv_scales_ready")
        M_hi_copied = sem("M_hi_copied")
        V_hi_copied = sem("V_hi_copied")
        pe_wT = sem("pe_wT")
        pe_ctxT = sem("pe_ctxT")
        pe_kq_heads = sem("pe_kq_heads")
        pe_v_head = sem("pe_v_head")
        pe_wo_b1 = sem("pe_wo_b1")
        pe_kv = sem("pe_kv")
        pe_M = sem("pe_M")
        pe_c = sem("pe_c")
        pe_V = sem("pe_V")
        pe_sgn = sem("pe_sgn")
        pe_alpha2 = sem("pe_alpha2")
        wT_copied = sem("wT_copied")
        wvT_copied = sem("wvT_copied")
        ctxT_copied = sem("ctxT_copied")
        kq_heads_copied = sem("kq_heads_copied")
        v_head_copied = sem("v_head_copied")
        wo_copied = sem("wo_copied")
        b1_copied = sem("b1_copied")
        khT_copied = sem("khT_copied")
        vhT_copied = sem("vhT_copied")
        M_copied = sem("M_copied")
        c_copied = sem("c_copied")
        V_copied = sem("V_copied")
        magnitudes1 = sem("magnitudes1")
        magnitudes2 = sem("magnitudes2")
        sgn_steps = sem("sgn_steps")
        sgn1_ready = sem("sgn1_ready")
        sgn2_ready = sem("sgn2_ready")
        sgn1T_copied = [sem(f"sgn1T_copied{k}") for k in range(KD)]
        sgn2T_copied = sem("sgn2T_copied")
        top_ready = sem("top_ready")
        top_reduced = sem("top_reduced")
        scale_steps = sem("scale_steps")
        alpha1_ready = sem("alpha1_ready")
        scales_ready = sem("scales_ready")
        diag2_ready = sem("diag2_ready")
        alpha2_ready = sem("alpha2_ready")

        x_loaded = [sem(f"x_loaded{n}") for n in range(2)]
        out_stored = [sem(f"out_stored{n}") for n in range(2)]
        raw_stats = [sem(f"raw_stats{n}") for n in range(2)]
        stats = [sem(f"stats{n}") for n in range(2)]
        norm_steps = [sem(f"norm_steps{n}") for n in range(2)]
        normed = [sem(f"normed{n}") for n in range(2)]
        x_turned = sem("x_turned")
        xT_hi_copied = sem("xT_hi_copied")
        xT_copied = sem("xT_copied")
        scored = sem("scored")
        sc_steps = sem("sc_steps")
        sc_maxed = sem("sc_maxed")
        exped = sem("exped")
        e_hi_done = sem("e_hi_done")
        e_split = sem("e_split")
        esum_used = sem("esum_used")
        einv_ready = sem("einv_ready")
        e_turned = sem("e_turned")
        eT_copied = sem("eT_copied")
        attended = sem("attended")
        x1_ready = sem("x1_ready")
        x1_turned = sem("x1_turned")
        hi_copied = sem("hi_copied")
        lo_copied = sem("lo_copied")
        y_ready = sem("y_ready")
        gelu_done = sem("gelu_done")
        hi_by_act = sem("hi_by_act")
        hi_by_pool = sem("hi_by_pool")
        h_lo_done = sem("h_lo_done")
        z_added = sem("z_added")
        z_scaled = sem("z_scaled")
        x1b_ready = sem("x1b_ready")
        out_ready = sem("out_ready")
        out_half_ready = sem("out_half_ready")

        wait_carrier = sem("wait_carrier")

        block = stack.enter_context(nc.Block())

        def val(i, par, per, n):
            return i * (2 * per) + (per * par + n)

        def dma_val(i, par):
            return i * 16 + 16 * (par // 2 + 1)

        def wait(eng, s, v):
            if not isinstance(v, int) or v > 0:
                eng.wait_ge(s, v)

        def wait_apart(eng, s, v):
            if not isinstance(v, int) or v > 0:
                eng.wait_ge(s, v)
                eng.sem_inc(wait_carrier, 1)

        def V_bank(n):
            return (psY + psZ + psZ)[n]

        def is_body(i, par, b):
            return isinstance(i, int) and 2 * i + par == b

        def has(i, par):
            return not isinstance(i, int) or 0 <= 2 * i + par < B

        def pipeline(eng, body, ahead=2):
            pairs = (B - ahead) // 2
            for b in range(-1, 2):
                body(b // 2, b % 2)
            with eng.Fori(1, pairs) as i:
                body(i, 0)
                body(i, 1)
            for b in range(2 * pairs, B + 1):
                body(b // 2, b % 2)

        @block.sync
        def _(sp):
            def rows(w):
                return w.rearrange("(k p) n -> p k n", p=P)

            def load_x(i, par):
                sp.dma_start(x_in[par % 2][:, :, :], x_v[i * 2 + par, :, :, :]) \
                  .then_inc(x_loaded[par % 2], 16)

            sp.dma_start(wk_sb[:, :, :], rows(Wk)).then_inc(loaded["wk"], 16)
            sp.dma_start(wq_sb[:, :, :], rows(Wq)).then_inc(loaded["wq"], 16)
            sp.dma_start(ctx_sb[:, :, :], ctx_in.rearrange("b t d -> (b t) d")
                         .rearrange("(n p) d -> p n d", p=P)).then_inc(loaded["ctx"], 16)
            sp.dma_start(wv_sb[:, :, :], rows(Wv)).then_inc(loaded["wv"], 16)
            load_x(0, 0)
            sp.dma_start(wo_sb[:, :, :], rows(Wo)).then_inc(loaded["wo"], 16)
            sp.dma_start(b1_row[:, :], b1.rearrange("(c p) -> c p", p=P)).then_inc(loaded["b1"], 16)
            sp.dma_start(w1_sb[:, :, :], rows(w1)).then_inc(loaded["w1"], 16)
            sp.dma_start(mask_sb[:, :, :], mask.rearrange("(p j) t -> p j t", p=P)) \
              .then_inc(loaded["mask"], 16)
            sp.dma_start(w2_sb[:, :, :], rows(w2)).then_inc(loaded["w2"], 16)
            load_x(0, 1)
            sp.dma_start(b2_bc[:, :], b2.rearrange("(a n) -> a n", a=1).to_broadcast([P, D])) \
              .then_inc(loaded["b2"], 16)

            def body(i, par):
                if has(i, par + 3):
                    wait(sp, x1_ready, val(i, par + 1, 1, 1))
                    load_x(i, par + 3)
                if is_body(i, par, B):
                    for n in range(2):
                        sp.wait_ge((out_ready, out_half_ready)[n], (B, 1)[n])
                        sp.dma_start(out_v[B - 1, :, 2 * n:2 * n + 2, :],
                                     z_sb[(B - 1) % 2][:, 2 * n:2 * n + 2, :]) \
                          .then_inc(out_stored[(B - 1) % 2], 16)
                elif has(i, par - 1):
                    wait(sp, out_ready, val(i, par - 1, 1, 1))
                    sp.dma_start(out_v[i * 2 + (par - 1), :, :, :], z_sb[(par - 1) % 2][:, :, :]) \
                      .then_inc(out_stored[(par - 1) % 2], 16)

            pipeline(sp, body, ahead=3)
            for n, s in enumerate(out_stored):
                sp.wait_ge(s, 16 * (B // 2 + n))

        @block.gpsimd
        def _(pool):
            nc.gpsimd.memset(ident[:, :], 0.0).then_inc(consts, 1)
            nc.gpsimd.memset(ident16[:, :], 0.0).then_inc(consts, 1)
            nc.gpsimd.memset(ones[:, :], 1.0).then_inc(consts, 1)
            nc.gpsimd.memset(mhalf[:, :], -0.5).then_inc(consts, 1)
            nc.gpsimd.memset(masked_sb[:, :, :], MASKED).then_inc(consts, 1)
            pool.wait_ge(consts, 2)
            for m in (ident, ident16):
                nc.gpsimd.affine_select(out=m[:, :], in_=m[:, :], compare_op=ALU.not_equal,
                                        fill=1.0, base=0, pattern=[[-1, P]],
                                        channel_multiplier=1).then_inc(identity, 1)
            pool.wait_ge(consts, 5)
            pool.wait_ge(identity, 2)
            nc.gpsimd.memset(wkvh[:, :, :], 0.0).then_inc(gaps_zeroed, 1)
            nc.gpsimd.memset(sel[:, :], 0.0).then_inc(gaps_zeroed, 1)
            nc.gpsimd.memset(mags[:, :], 0.0).then_inc(gaps_zeroed, 1)
            pool.wait_ge(gaps_zeroed, 3)

            def norm(i, par, n, src):
                wait_apart(pool, stats[n], val(i, par, 1, 1))
                nc.gpsimd.tensor_scalar(vare[n][:, :], st[n][:, :, 1], 1.0, EPS, ALU.mult, ALU.add) \
                    .then_inc(norm_steps[n], 1)
                nc.gpsimd.tensor_scalar(nmean[n][:, :], st[n][:, :, 0], -1.0, 1.0, ALU.mult,
                                        ALU.mult).then_inc(norm_steps[n], 1)
                wait(pool, norm_steps[n], val(i, par, 4, 2))
                nc.gpsimd.tensor_tensor(rstd[n][:, :], vare[n][:, :], mhalf[:, :], ALU.pow) \
                    .then_inc(norm_steps[n], 1)
                wait(pool, norm_steps[n], val(i, par, 4, 3))
                nc.gpsimd.tensor_tensor(nmr[n][:, :], nmean[n][:, :], rstd[n][:, :], ALU.mult) \
                    .then_inc(norm_steps[n], 1)
                wait(pool, (x_turned, x1_turned)[n], val(i, par - 1, KD, KD))
                wait_apart(pool, norm_steps[n], val(i, par, 4, 4))
                for j in range(T):
                    last = nc.gpsimd.tensor_scalar(xh[n][:, j, :], src[:, j, :],
                                                   rstd[n][:, j:j + 1], nmr[n][:, j:j + 1],
                                                   ALU.mult, ALU.add)
                last.then_inc(normed[n], 1)

            def top_of_hidden():
                pool.wait_ge(top_ready, 1)
                nc.gpsimd.partition_all_reduce(top_all[:, :], top[:, :], P,
                                               bass.bass_isa.ReduceOp.max).then_inc(top_reduced, 1)

            def hi(i, par, c):
                wait(pool, z_added, val(i, par, C, c - 3))
                wait_apart(pool, gelu_done, val(i, par, C, c + 1))
                nc.gpsimd.tensor_scalar(h_hi[c % 4][:, :], h_sb[c % 4][:, :], h_scale[:, :], 1.0,
                                        ALU.mult, ALU.mult).then_inc(hi_by_pool, 1)

            def body(i, par):
                if is_body(i, par, 0):
                    pool.wait_ge(scales_ready, 1)
                if has(i, par + 2) and not is_body(i, par, -1):
                    norm(i, par + 2, 0, x_in[par % 2])
                if has(i, par):
                    hi(i, par, 1)
                if has(i, par + 1):
                    norm(i, par + 1, 1, x1)
                if has(i, par):
                    hi(i, par, 5)
                    hi(i, par, 6)
                    hi(i, par, 7)
                if has(i, par - 1):
                    n = (par - 1) % 2
                    tiles = slice(0, 2) if is_body(i, par, B) else slice(0, T)
                    wait(pool, z_scaled, val(i, par - 1, 2, 1 if is_body(i, par, B) else 2))
                    wait(pool, x1b_ready, val(i, par - 1, 1, 1))
                    nc.gpsimd.tensor_tensor(z_sb[n][:, tiles, :], z_sb[n][:, tiles, :],
                                            x1b[n][:, tiles, :], ALU.add).then_inc(out_ready, 1)
                if has(i, par + 1):
                    n = (par + 1) % 2
                    wait(pool, x1_ready, val(i, par + 1, 1, 1))
                    wait(pool, out_ready, val(i, par - 1, 1, 1))
                    nc.gpsimd.tensor_tensor(x1b[n][:, :, :], x1[:, :, :],
                                            b2_bc[:, :].unsqueeze(1).to_broadcast([P, T, D]),
                                            ALU.add).then_inc(x1b_ready, 1)

            norm(0, 0, 0, x_in[0])
            pool.wait_ge(mags_ready, 4)
            nc.gpsimd.partition_all_reduce(mags_all[:, :], mags[:, :], P,
                                           bass.bass_isa.ReduceOp.max).then_inc(mags_reduced, 1)
            pool.wait_ge(mags_reduced, 1)
            norm(0, 1, 0, x_in[1])
            top_of_hidden()
            pool.wait_ge(loaded["b2"], 16)
            pipeline(pool, body)

        @block.scalar
        def _(act):
            act.dma_start(kh_sb[:, :, :], wk_h.rearrange("(k p) h -> p k h", p=P)).then_inc(loaded["kq_heads"], 16)
            act.dma_start(qh_sb[:, :, :], wq_h.rearrange("(k p) h -> p k h", p=P)).then_inc(loaded["kq_heads"], 16)
            act.dma_start(vh_sb[:, :, :], wv_h.rearrange("(k p) h -> p k h", p=P)).then_inc(loaded["v_head"], 16)
            for dst, src in ((bk_col[:, :], bk_h), (bv_col[V_AT:, :], bv_h), (bq_col[:, :], bq_h)):
                act.dma_start(dst, src.rearrange("(p a) -> p a", a=1)).then_inc(loaded["biases"], 16)

            def copy_V(n):
                act.wait_ge(pe_V, n + 1)
                nc.scalar.activation(V_hl[:, 2 * n:2 * n + 2, 0, :],
                                     V_bank(n)[:, :].rearrange("p (b d) -> p b d", b=2),
                                     ACT.Copy, scale=mv_scale[:, 1:2]).then_inc(V_hi_copied, 1)

            def exp(i, par):
                wait(act, sc_maxed, val(i, par, 1, 1))
                wait(act, e_split, val(i, par - 1, 1, 1))
                wait(act, esum_used, val(i, par - 1, 1, 1))
                for j in range(T):
                    last = nc.scalar.activation(e_sb[:, j, :], sc[:, j, :], ACT.Exp,
                                                bias=nmax[:, j:j + 1], scale=1.0,
                                                accum_out=esum[:, j:j + 1])
                last.then_inc(exped, 1)
                wait(act, exped, val(i, par, 1, 1))
                wait(act, e_turned, val(i, par - 1, 1, 1))
                nc.scalar.activation(e_hl[:, :, 0, :], e_sb[:, :, :], ACT.Copy,
                                     scale=E_SCALE).then_inc(e_hi_done, 1)

            def gelu(i, par, c):
                wait(act, y_ready, val(i, par, C, c + 1))
                wait(act, h_lo_done, val(i, par, C, c - 3))
                nc.scalar.activation(h_sb[c % 4][:, :], psY[c % 4][:, :], ACT.Gelu,
                                     bias=b1_col[:, c:c + 1], scale=alpha1x[:, c:c + 1]) \
                    .then_inc(gelu_done, 1)

            def hi(i, par, c):
                wait(act, gelu_done, val(i, par, C, c + 1))
                wait(act, z_added, val(i, par, C, c - 3))
                nc.scalar.activation(h_hi[c % 4][:, :], h_sb[c % 4][:, :], ACT.Copy,
                                     scale=h_scale[:, :]).then_inc(hi_by_act, 1)

            def copy_xT(i, par):
                wait(act, scored, val(i, par - 1, 1, 1))
                for k in range(KD):
                    wait(act, x_turned, val(i, par, KD, k + 1))
                    nc.scalar.activation(xT_hi[:, k, :], psW[k][:, :], ACT.Copy,
                                         scale=X_SCALE).then_inc(xT_hi_copied, 1)

            act.wait_ge(pe_wT, 3)
            nc.scalar.activation(wvT[:, :, :].rearrange("p k n -> p (k n)"), psY[2][:, :],
                                 ACT.Copy).then_inc(wvT_copied, 1)

            def copy_values(n):
                act.wait_ge(khT_copied, n + 1)
                for h in range(2):
                    nc.scalar.activation(vhT[V_AT:, n * (B // 2):(n + 1) * (B // 2), h, :],
                                         psY[n][V_AT:V_AT + HD, :].rearrange("p (b t) -> p b t", t=SK),
                                         ACT.Identity, bias=bv_col[V_AT:, :], scale=1.0) \
                        .then_inc(vhT_copied, 1)

            def copy_M(n):
                for k in range(KD):
                    m = n * KD + k
                    act.wait_ge(pe_M, m + 1)
                    nc.scalar.activation(M_hl[:, k, n * (B // 2):(n + 1) * (B // 2), 0, :],
                                         (psY[2], psY[3], psZ[0], psZ[1])[m][:, :]
                                         .rearrange("p (b t) -> p b t", t=SK),
                                         ACT.Copy, scale=mv_scale[:, 0:1]).then_inc(M_hi_copied, 1)

            def copy_c(n):
                act.wait_ge(pe_c, n + 1)
                nc.scalar.activation(c_sb[:, n * HALF:(n + 1) * HALF], psY[n][:, :],
                                     ACT.Copy).then_inc(c_copied, 1)

            copy_values(0)
            copy_xT(0, 0)
            act.wait_ge(mv_scales_ready, 1)
            copy_M(0)
            copy_c(0)
            copy_values(1)
            copy_M(1)
            act.wait_ge(loaded["w1"], 16)
            for c in range(C):
                last = nc.scalar.activation(magnitudes[:, c * D:(c + 1) * D], w1_sb[:, c, :], ACT.Abs,
                                            accum_out=abs1[:, c:c + 1])
            last.then_inc(magnitudes1, 1)
            copy_c(1)
            exp(0, 0)
            copy_V(0)

            def row_sums_2():
                act.wait_ge(loaded["w2"], 16)
                act.wait_ge(magnitudes1, 1)
                for k in range(KD):
                    last = nc.scalar.activation(magnitudes[:, k * H:(k + 1) * H], w2_sb[:, k, :], ACT.Abs,
                                                accum_out=abs2[:, k:k + 1])
                last.then_inc(magnitudes2, 1)

            def body(i, par):
                late, early, ffn = (has(i, par + d) for d in (1, 2, 0))
                if late:
                    wait(act, e_turned, val(i, par + 1, 1, 1))
                    wait(act, attended, val(i, par, 2, 2))
                    nc.scalar.activation(eT[:, :, :].rearrange("p j t -> p (j t)"),
                                         psW[0][:, :].bitcast(F16)[:, 0:T * P], ACT.Copy) \
                        .then_inc(eT_copied, 1)
                if is_body(i, par, -1):
                    copy_V(1)
                    row_sums_2()
                    copy_V(2)
                if is_body(i, par, 0):
                    act.wait_ge(alpha1_ready, 1)
                    act.wait_ge(b1_copied, 1)
                    act.wait_ge(scales_ready, 1)
                if ffn:
                    gelu(i, par, 0)
                    hi(i, par, 0)
                    gelu(i, par, 1)
                    gelu(i, par, 2)
                    gelu(i, par, 3)
                for b in range(2):
                    if is_body(i, par, b):
                        copy_V(4 + 2 * b)
                        copy_V(5 + 2 * b)
                if early:
                    copy_xT(i, par + 2)
                if is_body(i, par, -1):
                    copy_V(3)
                if ffn:
                    gelu(i, par, 4)
                    hi(i, par, 2)
                    hi(i, par, 3)
                    gelu(i, par, 5)
                    hi(i, par, 4)
                    gelu(i, par, 6)
                    gelu(i, par, 7)
                if late:
                    n = (par + 1) % 2
                    wait(act, y_ready, val(i, par - 1, C, C))
                    for m, k in enumerate(reversed(range(KD))):
                        wait(act, x1_turned, val(i, par + 1, KD, m + 1))
                        nc.scalar.activation(x_hi[n][:, k, :], psW[k][:, :], ACT.Copy,
                                             scale=X_SCALE).then_inc(hi_copied, 1)
                if is_body(i, par, -1):
                    act.wait_ge(pe_sgn, KD)
                    nc.scalar.activation(sgn1T[:, 1, :], psZ[1][:, :].bitcast(F16),
                                         ACT.Copy).then_inc(sgn1T_copied[1], 1)
                if early:
                    exp(i, par + 2)

            pipeline(act, body)

        @block.vector
        def _(dve):
            def raw_bn(n, src):
                for j in range(T):
                    last = nc.vector.bn_stats(st_raw[n][:, j, :], src[:, j, :])
                return last

            def bn(i, par, n):
                wait(dve, normed[n], val(i, par - 1, 1, 1))
                wait_apart(dve, raw_stats[n], val(i, par, 1, 1))
                for j in range(T):
                    last = nc.vector.bn_aggr(st[n][:, j, :], st_raw[n][:, j, :])
                last.then_inc(stats[n], 1)

            def lo(i, par, c):
                owner, chunks = (hi_by_act, ACT_HI) if c in ACT_HI else (hi_by_pool, POOL_HI)
                wait(dve, owner, val(i, par, len(chunks), chunks.index(c) + 1))
                nc.vector.scalar_tensor_tensor(out=h_lo[c % 4][:, :], in0=h_sb[c % 4][:, :],
                                               scalar=h_scale[:, :], in1=h_hi[c % 4][:, :],
                                               op0=ALU.mult, op1=ALU.subtract).then_inc(h_lo_done, 1)

            def scores(i, par):
                wait(dve, scored, val(i, par, 1, 1))
                wait(dve, exped, val(i, par - 1, 1, 1))
                b0 = i * (2 * SK) + par * SK
                ps = psW[0][:, :].rearrange("p (j n t) -> p j n t", j=T, n=2)
                nc.vector.scalar_tensor_tensor(
                    out=sc[:, :, :], in0=ps[:, :, 0, :], scalar=score_unscale[:, :],
                    in1=c_sb[:, bass.ds(b0, SK)].unsqueeze(1).to_broadcast([P, T, SK]),
                    op0=ALU.mult, op1=ALU.add).then_inc(sc_steps, 1)
                wait(dve, sc_steps, val(i, par, 3, 1))
                nc.vector.scalar_tensor_tensor(
                    out=sc[:, :, :], in0=ps[:, :, 1, :], scalar=score_unscale[:, :],
                    in1=sc[:, :, :], op0=ALU.mult, op1=ALU.add).then_inc(sc_steps, 1)

            def mask_and_max(i, par):
                wait_apart(dve, sc_steps, val(i, par, 3, 2))
                nc.vector.copy_predicated(sc[:, :, :], mask_sb[:, :, :], masked_sb[:, :, :]) \
                    .then_inc(sc_steps, 1)
                wait(dve, sc_steps, val(i, par, 3, 3))
                nc.vector.tensor_reduce(nmax[:, :], sc[:, :, :], AX.X, ALU.max, negate=True) \
                    .then_inc(sc_maxed, 1)

            def first_norm(i, par):
                n = par % 2
                wait(dve, x_loaded[n], dma_val(i, par))
                raw_bn(0, x_in[n]).then_inc(raw_stats[0], 1)
                bn(i, par, 0)

            def top_of_hidden():
                dve.wait_ge(b1_copied, 1)
                nc.vector.scalar_tensor_tensor(out=b1_abs[:, :], in0=b1_col[:, :], scalar=-1.0,
                                               in1=b1_col[:, :], op0=ALU.mult, op1=ALU.max) \
                    .then_inc(scale_steps, 1)
                dve.wait_ge(magnitudes1, 1)
                nc.vector.tensor_scalar(alpha1x[:, :], abs1[:, :], 1.0 / (D * X_SCALE), None,
                                        ALU.mult).then_inc(alpha1_ready, 1)
                dve.wait_ge(scale_steps, 1)
                nc.vector.scalar_tensor_tensor(out=bound[:, :], in0=abs1[:, :], scalar=1.001,
                                               in1=b1_abs[:, :], op0=ALU.mult, op1=ALU.add) \
                    .then_inc(scale_steps, 1)
                dve.wait_ge(scale_steps, 2)
                nc.vector.tensor_reduce(top[:, :], bound[:, :], AX.X, ALU.max).then_inc(top_ready, 1)

            def minus_where_negative(neg, w_flat):
                nc.vector.tensor_scalar(neg[:, :], w_flat, 0.0, None, ALU.is_lt).then_inc(sgn_steps, 1)

            def signs(sgn, neg, w_flat, step, ready):
                dve.wait_ge(sgn_steps, step)
                nc.vector.scalar_tensor_tensor(out=sgn[:, :], in0=w_flat, scalar=0.0, in1=neg[:, :],
                                               op0=ALU.is_gt, op1=ALU.subtract).then_inc(ready, 1)

            def split_xT(i, par):
                for k in range(KD):
                    wait(dve, xT_hi_copied, val(i, par, KD, k + 1))
                    nc.vector.scalar_tensor_tensor(out=xT_lo[:, k, :], in0=psW[k][:, :], scalar=X_SCALE,
                                                   in1=xT_hi[:, k, :], op0=ALU.mult,
                                                   op1=ALU.subtract).then_inc(xT_copied, 1)

            def copy_V(n):
                dve.wait_ge(V_hi_copied, n + 1)
                nc.vector.scalar_tensor_tensor(
                    out=V_hl[:, 2 * n:2 * n + 2, 1, :],
                    in0=V_bank(n)[:, :].rearrange("p (b d) -> p b d", b=2),
                    scalar=mv_scale[:, 1:2], in1=V_hl[:, 2 * n:2 * n + 2, 0, :],
                    op0=ALU.mult, op1=ALU.subtract).then_inc(V_copied, 1)

            w1_flat = w1_sb[:, :, :].rearrange("p c d -> p (c d)")
            w2_flat = w2_sb[:, :, :].rearrange("p k n -> p (k n)")

            dve.wait_ge(identity, 1)
            dve.wait_ge(gaps_zeroed, 3)
            nc.vector.tensor_reduce(sel[:, V_AT:], ident[:, :].rearrange("p (g h) -> p h g", h=HD),
                                    AX.X, ALU.add).then_inc(sel_ready, 1)
            for n, w in enumerate((wkT, wqT)):
                dve.wait_ge(pe_wT, n + 1)
                nc.vector.tensor_copy(w[:, :, :].rearrange("p k n -> p (k n)"), psY[n][:, :]) \
                    .then_inc(wT_copied, 1)
            dve.wait_ge(pe_kq_heads, 1)
            nc.vector.tensor_copy(wkvh[:, :, 0:HD], psY[3][:, D:D + KD * HD]
                                  .rearrange("p (k h) -> p k h", k=KD)).then_inc(kq_heads_copied, 1)
            nc.vector.tensor_copy(wqhT[:, :], psY[3][0:HD, 0:D]).then_inc(kq_heads_copied, 1)
            for k in range(KD):
                for n in range(NH):
                    m = k * NH + n
                    dve.wait_ge(pe_ctxT, m + 1)
                    nc.vector.tensor_copy(ctxT[:, k, n * HALF:(n + 1) * HALF],
                                          (psZ[0], psZ[1], psW[0], psW[1])[m][:, :]) \
                        .then_inc(ctxT_copied, 1)
            first_norm(0, 0)
            dve.wait_ge(loaded["biases"], 48)
            dve.wait_ge(consts, 5)
            nc.vector.tensor_scalar(bq_rep[:, :], ones[0:HD, :], bq_col[:, :], None,
                                    ALU.mult).then_inc(bq_ready, 1)
            for rows, b in ((slice(0, HD), bk_col[:, :]), (slice(V_AT, V_AT + HD), bv_col[V_AT:, :])):
                nc.vector.scalar_tensor_tensor(out=bias_abs[rows, :], in0=b, scalar=-1.0, in1=b,
                                               op0=ALU.mult, op1=ALU.max).then_inc(bias_abs_ready, 1)
            dve.wait_ge(pe_v_head, 1)
            nc.vector.tensor_copy(wkvh[:, :, V_AT:], psY[1][:, 0:KD * HD]
                                  .rearrange("p (k h) -> p k h", k=KD)).then_inc(v_head_copied, 1)
            dve.wait_ge(pe_wo_b1, 1)
            nc.vector.tensor_copy(wo_sum[V_AT:, :], psW[0][V_AT:V_AT + HD, 0:D]).then_inc(wo_copied, 1)
            nc.vector.tensor_copy(b1_col[:, :], psW[0][:, D:D + C]).then_inc(b1_copied, 1)
            dve.wait_ge(kq_heads_copied, 2)
            dve.wait_ge(wo_copied, 1)
            for col, src, at in ((2, wqhT[:, :], 0), (3, wo_sum[V_AT:, :], V_AT)):
                nc.vector.tensor_reduce(mags[at:at + HD, col:col + 1], src, AX.X, ALU.max,
                                        apply_absolute_value=True).then_inc(mags_ready, 1)
            dve.wait_ge(loaded["w1"], 16)
            minus_where_negative(neg1, w1_flat)

            def largest_kv(n):
                dve.wait_ge(pe_kv, n + 1)
                nc.vector.tensor_reduce(kv_max[:, n:n + 1], psY[n][0:V_AT + HD, :], AX.X, ALU.max,
                                        apply_absolute_value=True).then_inc(kv_maxed, 1)

            def copy_keys(n):
                nc.vector.tensor_scalar(khT[:, n * HALF:(n + 1) * HALF], psY[n][0:HD, :],
                                        bk_col[:, :], SCORE_SCALE, ALU.add, ALU.mult) \
                    .then_inc(khT_copied, 1)

            largest_kv(0)
            copy_keys(0)
            largest_kv(1)
            dve.wait_ge(kv_maxed, NH)
            nc.vector.tensor_tensor(kv_max[:, NH:], kv_max[:, 0:1], kv_max[:, 1:2], ALU.max) \
                .then_inc(kv_maxed, 1)
            dve.wait_ge(kv_maxed, NH + 1)
            dve.wait_ge(bias_abs_ready, 2)
            for col, scale in ((0, SCORE_SCALE), (1, 1.0)):
                rows = slice(col * V_AT, col * V_AT + HD)
                nc.vector.tensor_scalar(mags[rows, col:col + 1], kv_max[rows, NH:], bias_abs[rows, :],
                                        scale, ALU.add, ALU.mult).then_inc(mags_ready, 1)
            copy_keys(1)
            dve.wait_ge(mags_reduced, 1)
            nc.vector.tensor_tensor(mv_bound[:, :], mags_all[:, 0:2], mags_all[:, 2:4], ALU.mult) \
                .then_inc(mv_steps, 1)
            dve.wait_ge(mv_steps, 1)
            nc.vector.tensor_scalar(mv_bound[:, :], mv_bound[:, :], LEAST_BOUND, None, ALU.max) \
                .then_inc(mv_steps, 1)
            dve.wait_ge(mv_steps, 2)
            nc.vector.tensor_scalar(mv_pow2[:, :].bitcast(U32), mv_bound[:, :].bitcast(U32), 0x7F800000,
                                    None, ALU.bitwise_and).then_inc(mv_steps, 1)
            dve.wait_ge(mv_steps, 3)
            nc.vector.reciprocal(mv_inv[:, :], mv_pow2[:, :]).then_inc(mv_steps, 1)
            nc.vector.tensor_scalar(score_unscale[:, :], mv_pow2[:, 0:1], 1.0 / (MV_TOP * X_SCALE), None,
                                    ALU.mult).then_inc(mv_steps, 1)
            dve.wait_ge(mv_steps, 5)
            nc.vector.tensor_scalar(mv_scale[:, :], mv_inv[:, :], MV_TOP, None,
                                    ALU.mult).then_inc(mv_scales_ready, 1)
            dve.wait_ge(mv_scales_ready, 1)
            split_xT(0, 0)
            for m, (k, n) in enumerate((k, n) for n in range(NH) for k in range(KD)):
                dve.wait_ge(M_hi_copied, m + 1)
                part = M_hl[:, k, n * (B // 2):(n + 1) * (B // 2), :, :]
                nc.vector.scalar_tensor_tensor(
                    out=part[:, :, 1, :], in0=(psY[2], psY[3], psZ[0], psZ[1])[m][:, :]
                    .rearrange("p (b t) -> p b t", t=SK), scalar=mv_scale[:, 0:1],
                    in1=part[:, :, 0, :], op0=ALU.mult, op1=ALU.subtract).then_inc(M_copied, 1)
            dve.wait_ge(c_copied, 1)
            dve.wait_ge(loaded["mask"], 16)
            scores(0, 0)
            mask_and_max(0, 0)
            first_norm(0, 1)

            def hidden_scales():
                dve.wait_ge(top_reduced, 1)
                nc.vector.tensor_scalar(top[:, :], top_all[:, :], LEAST_BOUND, None, ALU.max) \
                    .then_inc(scale_steps, 1)
                dve.wait_ge(scale_steps, 3)
                nc.vector.tensor_scalar(pow2[:, :].bitcast(U32), top[:, :].bitcast(U32), 0x7F800000,
                                        None, ALU.bitwise_and).then_inc(scale_steps, 1)
                dve.wait_ge(scale_steps, 4)
                nc.vector.reciprocal(inv_pow2[:, :], pow2[:, :]).then_inc(scale_steps, 1)
                nc.vector.tensor_scalar(h_unscale[:, :], pow2[:, :], 1.0 / H_TOP, None,
                                        ALU.mult).then_inc(scale_steps, 1)
                dve.wait_ge(scale_steps, 6)
                nc.vector.tensor_scalar(h_scale[:, :], inv_pow2[:, :], H_TOP, None,
                                        ALU.mult).then_inc(scales_ready, 1)

            def diagonals():
                dve.wait_ge(magnitudes2, 1)
                for k in range(KD):
                    nc.vector.tensor_scalar(diag2[:, k, :], ident[:, :], abs2[:, k:k + 1], 1.0 / H,
                                            ALU.mult, ALU.mult).then_inc(diag2_ready, 1)

            def copy_signs_2():
                for n in range(2):
                    dve.wait_ge(pe_sgn, KD + n + 1)
                    nc.vector.tensor_copy(sgn2T[:, 4 * n:4 * n + 4, :].rearrange("p c d -> p (c d)"),
                                          psZ[n][:, :].bitcast(F16)).then_inc(sgn2T_copied, 1)

            def scale_alpha2():
                dve.wait_ge(scales_ready, 1)
                dve.wait_ge(pe_alpha2, 1)
                nc.vector.tensor_scalar(alpha2_bc[:, :], psZ[0][:, 0:D], h_unscale[:, :], None,
                                        ALU.mult).then_inc(alpha2_ready, 1)

            def body(i, par):
                late, early, ffn, prev = (has(i, par + d) for d in (1, 2, 0, -1))
                if prev:
                    lo(i, par - 1, 6)
                    lo(i, par - 1, 7)
                if late:
                    wait(dve, exped, val(i, par + 1, 1, 1))
                    nc.vector.tensor_scalar(esum_scaled[:, :], esum[:, :], mv_scale[:, 1:2], E_SCALE,
                                            ALU.mult, ALU.mult).then_inc(esum_used, 1)
                    wait(dve, esum_used, val(i, par + 1, 1, 1))
                    nc.vector.reciprocal(einv[:, :], esum_scaled[:, :]).then_inc(einv_ready, 1)
                    wait(dve, e_hi_done, val(i, par + 1, 1, 1))
                    nc.vector.scalar_tensor_tensor(out=e_hl[:, :, 1, :], in0=e_sb[:, :, :],
                                                   scalar=E_SCALE, in1=e_hl[:, :, 0, :],
                                                   op0=ALU.mult, op1=ALU.subtract).then_inc(e_split, 1)
                if early and not is_body(i, par, -1):
                    first_norm(i, par + 2)
                if is_body(i, par, -1):
                    copy_V(0)
                    dve.wait_ge(loaded["w2"], 16)
                    minus_where_negative(neg2, w2_flat)
                    copy_V(1)
                    top_of_hidden()
                if is_body(i, par, 0):
                    diagonals()
                    signs(sgn2, neg2, w2_flat, 2, sgn2_ready)
                    scale_alpha2()
                if prev:
                    m = (par - 1) % 2
                    wait(dve, z_added, val(i, par - 1, C, C))
                    if is_body(i, par, 1):
                        dve.wait_ge(alpha2_ready, 1)
                    wait(dve, out_stored[m], dma_val(i, par - 3))
                    for n in range(2):
                        nc.vector.tensor_tensor(
                            z_sb[m][:, 2 * n:2 * n + 2, :],
                            psZ[n][:, :].rearrange("p (j d) -> p j d", j=2),
                            alpha2_bc[:, :].unsqueeze(1).to_broadcast([P, 2, D]), ALU.mult) \
                            .then_inc(z_scaled, 1)
                if is_body(i, par, B):
                    m = (B - 1) % 2
                    dve.wait_ge(z_scaled, 2 * B)
                    dve.wait_ge(x1b_ready, B)
                    nc.vector.tensor_tensor(z_sb[m][:, 2:4, :], z_sb[m][:, 2:4, :], x1b[m][:, 2:4, :],
                                            ALU.add).then_inc(out_half_ready, 1)
                if late:
                    m = (par + 1) % 2
                    wait(dve, einv_ready, val(i, par + 1, 1, 1))
                    wait(dve, x1b_ready, val(i, par, 1, 1))
                    for j in range(T):
                        if j % 2 == 0:
                            wait(dve, attended, val(i, par + 1, 2, j // 2 + 1))
                        last = nc.vector.scalar_tensor_tensor(
                            out=x1[:, j, :], in0=psW[j // 2][:, (j % 2) * D:(j % 2 + 1) * D],
                            scalar=einv[:, j:j + 1], in1=x_in[m][:, j, :], op0=ALU.mult, op1=ALU.add)
                    last.then_inc(x1_ready, 1)
                    wait(dve, x1_ready, val(i, par + 1, 1, 1))
                    raw_bn(1, x1).then_inc(raw_stats[1], 1)
                    bn(i, par + 1, 1)
                if ffn:
                    lo(i, par, 0)
                for b in range(2):
                    if is_body(i, par, b):
                        copy_V(4 + 2 * b)
                        copy_V(5 + 2 * b)
                if early:
                    split_xT(i, par + 2)
                if is_body(i, par, 0):
                    copy_signs_2()
                if is_body(i, par, -1):
                    signs(sgn1, neg1, w1_flat, 1, sgn1_ready)
                if ffn:
                    lo(i, par, 1)
                    lo(i, par, 2)
                    lo(i, par, 3)
                if early:
                    scores(i, par + 2)
                if ffn:
                    lo(i, par, 4)
                if early:
                    mask_and_max(i, par + 2)
                if is_body(i, par, -1):
                    copy_V(2)
                    dve.wait_ge(pe_sgn, 1)
                    nc.vector.tensor_copy(sgn1T[:, 0, :], psZ[0][:, :].bitcast(F16)) \
                        .then_inc(sgn1T_copied[0], 1)
                if ffn:
                    lo(i, par, 5)
                if late:
                    m = (par + 1) % 2
                    for n, k in enumerate(reversed(range(KD))):
                        wait(dve, hi_copied, val(i, par + 1, KD, n + 1))
                        nc.vector.scalar_tensor_tensor(out=x_lo[m][:, k, :], in0=psW[k][:, :],
                                                       scalar=X_SCALE, in1=x_hi[m][:, k, :],
                                                       op0=ALU.mult, op1=ALU.subtract) \
                            .then_inc(lo_copied, 1)
                if is_body(i, par, -1):
                    copy_V(3)
                    hidden_scales()

            pipeline(dve, body)

        @block.tensor
        def _(pe):
            def turn_square(n, w, name):
                pe.wait_ge(loaded[name], 16)
                for k in range(KD):
                    for m in range(KD):
                        last = nc.tensor.transpose(psY[n][:, k * D + m * P:k * D + (m + 1) * P],
                                                   w[:, m, k * P:(k + 1) * P], ident[:, :])
                last.then_inc(pe_wT, 1)

            def turn_context():
                pe.wait_ge(loaded["ctx"], 16)
                for k in range(KD):
                    for h in range(NH):
                        ps = (psZ[0], psZ[1], psW[0], psW[1])[k * NH + h]
                        for t in range(HALF // P):
                            last = nc.tensor.transpose(ps[:, t * P:(t + 1) * P],
                                                       ctx_sb[:, h * (HALF // P) + t, k * P:(k + 1) * P],
                                                       ident[:, :])
                        last.then_inc(pe_ctxT, 1)

            def key_and_query_heads():
                pe.wait_ge(loaded["kq_heads"], 32)
                pe.wait_ge(wT_copied, 1)
                for m in range(KD):
                    at = D + m * HD
                    for k in range(KD):
                        nc.tensor.matmul(psY[3][:, at:at + HD], wkT[:, k, m * P:(m + 1) * P],
                                         kh_sb[:, k, :], start=(k == 0), stop=(k == KD - 1))
                pe.wait_ge(wT_copied, 2)
                for k in range(KD):
                    last = nc.tensor.matmul(psY[3][0:HD, 0:D], qh_sb[:, k, :], wqT[:, k, :],
                                            start=(k == 0), stop=(k == KD - 1))
                last.then_inc(pe_kq_heads, 1)

            def value_head():
                pe.wait_ge(loaded["v_head"], 16)
                pe.wait_ge(wvT_copied, 1)
                for m in range(KD):
                    for k in range(KD):
                        last = nc.tensor.matmul(psY[1][:, m * HD:(m + 1) * HD], wvT[:, k, m * P:(m + 1) * P],
                                                vh_sb[:, k, :], start=(k == 0), stop=(k == KD - 1))
                last.then_inc(pe_v_head, 1)

            def wo_blocks_and_b1():
                pe.wait_ge(sel_ready, 1)
                pe.wait_ge(loaded["wo"], 16)
                pe.wait_ge(loaded["b1"], 16)
                pe.wait_ge(ctxT_copied, 3)
                for k in range(KD):
                    nc.tensor.matmul(psW[0][0:V_AT + HD, 0:D], sel[:, :], wo_sb[:, k, :],
                                     start=(k == 0), stop=(k == KD - 1))
                nc.tensor.transpose(psW[0][:, D:D + C], b1_row[:, :], ident[0:C, 0:C]).then_inc(pe_wo_b1, 1)

            def keys_and_values():
                pe.wait_ge(kq_heads_copied, 2)
                pe.wait_ge(v_head_copied, 1)
                pe.wait_ge(ctxT_copied, 4)
                for n in range(NH):
                    for k in range(KD):
                        last = nc.tensor.matmul(psY[n][0:V_AT + HD, :], wkvh[:, k, :],
                                                ctxT[:, k, n * HALF:(n + 1) * HALF],
                                                start=(k == 0), stop=(k == KD - 1))
                    last.then_inc(pe_kv, 1)

            def score_weights(n):
                pe.wait_ge(khT_copied, n + 1)
                for k in range(KD):
                    nc.tensor.matmul((psY[2], psY[3], psZ[0], psZ[1])[n * KD + k][:, :],
                                     wqhT[:, k * P:(k + 1) * P], khT[:, n * HALF:(n + 1) * HALF],
                                     start=True, stop=True).then_inc(pe_M, 1)

            def score_constants(n):
                pe.wait_ge(bq_ready, 1)
                pe.wait_ge(vhT_copied, 2 * n + 2)
                nc.tensor.matmul(psY[n][:, :], bq_rep[:, :], khT[:, n * HALF:(n + 1) * HALF],
                                 start=True, stop=True).then_inc(pe_c, 1)

            def values(n):
                if n < NH:
                    if n == 0:
                        pe.wait_ge(wo_copied, 1)
                        pe.wait_ge(vhT_copied, 4)
                    pe.wait_ge(c_copied, n + 1)
                elif n < 4:
                    pe.wait_ge(M_copied, n - 1)
                elif n < 6:
                    pe.wait_ge(sgn1T_copied[n - 4], 1)
                    pe.wait_ge(alpha2_ready, 1)
                else:
                    pe.wait_ge(z_scaled, 2)
                for m in range(2):
                    last = nc.tensor.matmul(V_bank(n)[:, m * D:(m + 1) * D],
                                            vhT[V_AT:, 2 * n + m, :, :].rearrange("p h t -> p (h t)"),
                                            wo_sum[V_AT:, :], start=True, stop=True)
                last.then_inc(pe_V, 1)

            def turn_signs_1():
                pe.wait_ge(sgn1_ready, 1)
                pe.wait_ge(M_copied, 4)
                for k in range(KD):
                    ps = psZ[k][:, :].bitcast(F16)
                    for c in range(C):
                        last = nc.tensor.transpose(ps[:, c * P:(c + 1) * P],
                                                   sgn1[:, c * D + k * P:c * D + (k + 1) * P], ident16[:, :])
                    last.then_inc(pe_sgn, 1)

            def turn_signs_2():
                pe.wait_ge(sgn2_ready, 1)
                pe.wait_ge(V_copied, 6)
                for n in range(2):
                    ps = psZ[n][:, :].bitcast(F16)
                    for c in range(4):
                        for k in range(KD):
                            a = k * H + (4 * n + c) * P
                            last = nc.tensor.transpose(ps[:, c * D + k * P:c * D + (k + 1) * P],
                                                       sgn2[:, a:a + P], ident16[:, :])
                    last.then_inc(pe_sgn, 1)

            def sum_alpha2():
                pe.wait_ge(diag2_ready, 2)
                pe.wait_ge(sgn1T_copied[0], 1)
                for k in range(KD):
                    last = nc.tensor.matmul(psZ[0][:, k * P:(k + 1) * P], ones[:, :], diag2[:, k, :],
                                            start=True, stop=True)
                last.then_inc(pe_alpha2, 1)

            def turn_x(i, par, n):
                wait(pe, normed[n], val(i, par, 1, 1))
                if n == 0:
                    wait(pe, x1_ready, val(i, par - 1, 1, 1))
                else:
                    wait(pe, xT_copied, val(i, par + 1, KD, KD) if has(i, par + 1) else 0)
                    wait(pe, x1_ready, val(i, par, 1, 1))
                for k in (range(KD) if n == 0 else reversed(range(KD))):
                    if n == 1 and k == 0 and has(i, par + 1):
                        wait(pe, sc_steps, val(i, par + 1, 3, 2))
                    for j in range(T):
                        last = nc.tensor.transpose(psW[k][:, j * P:(j + 1) * P],
                                                   xh[n][:, j, k * P:(k + 1) * P], ident[:, :])
                    last.then_inc((x_turned, x1_turned)[n], 1)

            def score(i, par):
                wait(pe, xT_copied, val(i, par, KD, KD))
                for j in range(T):
                    for n, (k, part) in enumerate((k, part) for k in range(KD) for part in (xT_hi, xT_lo)):
                        last = nc.tensor.matmul(psW[0][:, j * 2 * SK:(j + 1) * 2 * SK],
                                                part[:, k, j * P:(j + 1) * P],
                                                M_hl[:, k, i * 2 + par, :, :].rearrange("p n t -> p (n t)"),
                                                start=(n == 0), stop=(n == 2 * KD - 1))
                last.then_inc(scored, 1)

            def turn_e(i, par):
                wait(pe, e_split, val(i, par, 1, 1))
                wait(pe, lo_copied, val(i, par - 1, KD, KD))
                ps = psW[0][:, :].bitcast(F16)
                for j in range(T):
                    last = nc.tensor.transpose(ps[:, j * P:(j + 1) * P],
                                               e_hl[:, j, :, :].rearrange("p n t -> p (n t)"),
                                               ident16[:, :])
                last.then_inc(e_turned, 1)

            def attend(i, par):
                wait(pe, eT_copied, val(i, par, 1, 1))
                wait(pe, lo_copied, val(i, par - 1, KD, KD))
                wait(pe, xT_copied, val(i, par, KD, KD))
                for j in range(T):
                    for n in range(2):
                        last = nc.tensor.matmul(psW[j // 2][:, (j % 2) * D:(j % 2 + 1) * D],
                                                eT[:, j, :], V_hl[:, i * 2 + par, n, :],
                                                start=(n == 0), stop=(n == 1))
                    if j % 2:
                        last.then_inc(attended, 1)

            def first_product(i, par, c):
                if c == 0:
                    wait(pe, lo_copied, val(i, par, KD, KD))
                if is_body(i, par, 0) and c < 4:
                    pe.wait_ge(V_copied, c + 1)
                wait(pe, gelu_done, val(i, par, C, c - 3))
                slot = par % 2
                n = 0
                for k in range(KD):
                    for part in (x_hi, x_lo):
                        last = nc.tensor.matmul(psY[c % 4][:, :], sgn1T[:, k, c * P:(c + 1) * P],
                                                part[slot][:, k, :], start=(n == 0), stop=(n == 2 * KD - 1))
                        n += 1
                last.then_inc(y_ready, 1)

            def second_product(i, par, c):
                wait(pe, h_lo_done, val(i, par, C, c + 1))
                if c == 0:
                    wait(pe, z_scaled, val(i, par - 1, 2, 2))
                for j in range(T):
                    for n, part in enumerate((h_hi, h_lo)):
                        last = nc.tensor.matmul(psZ[j // 2][:, (j % 2) * D:(j % 2 + 1) * D],
                                                part[c % 4][:, j * P:(j + 1) * P], sgn2T[:, c, :],
                                                start=(c == 0 and n == 0 and j % 2 == 0),
                                                stop=(c == C - 1 and n == 1 and j % 2 == 1))
                last.then_inc(z_added, 1)

            def body(i, par):
                late, early, ffn, prev = (has(i, par + d) for d in (1, 2, 0, -1))
                if is_body(i, par, 0):
                    for k in range(KD):
                        pe.wait_ge(sgn1T_copied[k], 1)
                if ffn:
                    first_product(i, par, 0)
                if prev:
                    for c in range(C - TAIL, C):
                        second_product(i, par - 1, c)
                if late:
                    turn_e(i, par + 1)
                if ffn:
                    first_product(i, par, 1)
                if is_body(i, par, -1):
                    pe.wait_ge(V_copied, 1)
                if late:
                    attend(i, par + 1)
                if is_body(i, par, 0):
                    sum_alpha2()
                if is_body(i, par, -1):
                    values(2)
                if ffn:
                    first_product(i, par, 2)
                    first_product(i, par, 3)
                for b in range(2):
                    if is_body(i, par, b):
                        values(4 + 2 * b)
                        values(5 + 2 * b)
                if ffn:
                    first_product(i, par, 4)
                    first_product(i, par, 5)
                if early:
                    turn_x(i, par + 2, 0)
                if is_body(i, par, -1):
                    values(3)
                if ffn:
                    first_product(i, par, 6)
                if is_body(i, par, 0):
                    turn_signs_2()
                if ffn:
                    first_product(i, par, 7)
                    if is_body(i, par, 0):
                        pe.wait_ge(sgn2T_copied, 2)
                    if is_body(i, par, 1):
                        pe.wait_ge(V_copied, B // 2)
                    second_product(i, par, 0)
                if early:
                    score(i, par + 2)
                if is_body(i, par, -1):
                    turn_signs_1()
                if ffn:
                    second_product(i, par, 1)
                    second_product(i, par, 2)
                if late:
                    turn_x(i, par + 1, 1)
                if ffn:
                    for c in range(3, C - TAIL):
                        second_product(i, par, c)

            pe.wait_ge(identity, 2)
            pe.wait_ge(consts, 5)
            turn_square(0, wk_sb, "wk")
            turn_square(1, wq_sb, "wq")
            key_and_query_heads()
            turn_context()
            turn_square(2, wv_sb, "wv")
            value_head()
            wo_blocks_and_b1()
            keys_and_values()
            pe.wait_ge(wo_copied, 1)
            pe.wait_ge(b1_copied, 1)
            turn_x(0, 0, 0)
            score_weights(0)
            score_constants(0)
            score_weights(1)
            pe.wait_ge(M_copied, 2)
            score(0, 0)
            score_constants(1)
            values(0)
            values(1)
            pipeline(pe, body)


_INS = ['x', 'ctx_1024', 'mask_SxS2_bk1', 'L0_xattn_Wq', 'L0_xattn_Wk', 'L0_xattn_Wv', 'L0_xattn_wq_h',
        'L0_xattn_bq_h', 'L0_xattn_wk_h', 'L0_xattn_bk_h', 'L0_xattn_wv_h', 'L0_xattn_bv_h',
        'L0_xattn_Wo', 'L0_ffn_w1', 'L0_ffn_b1', 'L0_ffn_w2', 'L0_ffn_b2']


def kernel(**inputs):
    import numpy as _np
    import concourse.bacc as _bacc
    from concourse import mybir as _mybir
    from concourse.bass_utils import run_bass_kernel_spmd as _run

    nc = _bacc.Bacc("TRN2", target_bir_lowering=False, num_devices=1)
    arrays, args = {}, []
    for name in _INS:
        a = _np.ascontiguousarray(inputs[name])
        arrays[f"in_{name}"] = a
        args.append(nc.dram_tensor(f"in_{name}", a.shape, _mybir.dt.from_np(a.dtype), kind="ExternalInput").ap())
    out = nc.dram_tensor("out_x", arrays["in_x"].shape, _mybir.dt.float32, kind="ExternalOutput").ap()
    xattn_ffn_kernel(nc, *args, out)
    r = _run(nc, [arrays], core_ids=[0])
    return r.results[0]["out_x"]
```
